# Optimizing a Trainium2 kernel written in Bass

```python
import numpy as np
import jax
import jax.numpy as jnp

def _softmax(x, axis=-1):
    return jax.nn.softmax(x, axis=axis)

def _gelu(x):
    return jax.nn.gelu(x, approximate=True)

def _silu(x):
    return jax.nn.silu(x)

def _sigmoid(x):
    return jax.nn.sigmoid(x)

def _layernorm(x, axis=-1, eps=1e-05):
    m = jnp.mean(x, axis=axis, keepdims=True)
    v = jnp.var(x, axis=axis, keepdims=True)
    return (x - m) / jnp.sqrt(v + eps)

def _scatter_add(tgt, idx, src, axis=0):
    return tgt.at[idx].add(src)

def _segment_sum(src, seg, n):
    return jax.ops.segment_sum(src, seg, n)
kernel_name = 'mk_early_fusion_embed_d1_tok_img512_r4_3cd7f2'

def setup_inputs(seed: int=0):
    np.random.seed(seed)
    _w = jnp.asarray

    def _rec_inputs():
        import jax
        import jax.numpy as jnp
        _rk = jax.random.key(seed)
        x = -0.000356955 + 1 * jax.random.normal(jax.random.fold_in(_rk, 1), (8, 3, 224, 224), jnp.float32)
        x_txt = jax.random.randint(jax.random.fold_in(_rk, 51), (8, 512), 0, 12564, jnp.int32)
        return (x, x_txt)
    x, x_txt = _rec_inputs()

    def _L0_tok_setup():
        import jax, jax.numpy as jnp
        import numpy as np
        key = jax.random.key(seed)
        k1, k2, k3 = jax.random.split(key, 3)
        B, C, H, W = (128, 3, 224, 224)
        E, p = (128, 16)
        K = C * p * p
        img = jax.random.normal(k1, (B, C, H, W), dtype=jnp.float32)
        w = jax.random.normal(k2, (E, K), dtype=jnp.float32) * (1.0 / np.sqrt(K))
        b = jax.random.normal(k3, (E,), dtype=jnp.float32)
        return {'img': img, 'w': w, 'b': b, 'patch_size': p}
    _L0_tok_all = _L0_tok_setup()
    _L0_tok_in = {k: v for k, v in _L0_tok_all.items() if k in ('w', 'b')}
    del _L0_tok_all

    def _L0_txt_setup():
        import jax, jax.numpy as jnp
        import numpy as np
        VOCAB = 50257
        D_MODEL = 128
        B, S = (4, 1024)
        key = jax.random.key(seed)
        k_ids, k_w = jax.random.split(key)
        token_ids = jax.random.randint(k_ids, (B, S), 0, VOCAB, dtype=jnp.int64 if jax.config.jax_enable_x64 else jnp.int32)
        w = jax.random.truncated_normal(k_w, -3.0, 3.0, (VOCAB, D_MODEL), dtype=jnp.float32)
        return {'token_ids': token_ids, 'w': w}
    _L0_txt_all = _L0_txt_setup()
    _L0_txt_in = {k: v for k, v in _L0_txt_all.items() if k in ('w',)}
    del _L0_txt_all

    def _L0_attn_setup():
        import jax, jax.numpy as jnp
        import numpy as np
        DIM = 128
        HEADS = 8
        HEAD_DIM = DIM // HEADS

        def sinusoidal_pe(length, d_model):
            pos = jnp.arange(length, dtype=jnp.float32)[:, None]
            div = jnp.exp(jnp.arange(0, d_model, 2, dtype=jnp.float32) * (-jnp.log(jnp.float32(10000.0)) / d_model))
            ang = pos * div
            return jnp.stack([jnp.sin(ang), jnp.cos(ang)], axis=-1).reshape(length, d_model)

        def relative_shift(pos_score):
            B, H, N, M = pos_score.shape
            padded = jnp.pad(pos_score, ((0, 0), (0, 0), (0, 0), (1, 0)))
            padded = padded.reshape(B, H, M + 1, N)
            return padded[:, :, 1:].reshape(B, H, N, M)
        key = jax.random.key(seed)
        ks = jax.random.split(key, 7)
        B, N = (8, 256)
        s = lambda fan: 1.0 / np.sqrt(fan)
        x = jax.random.normal(ks[0], (B, N, DIM), dtype=jnp.float32)
        Wqkv = jax.random.normal(ks[1], (DIM, 3 * DIM), dtype=jnp.float32) * s(DIM)
        Wpos = jax.random.normal(ks[2], (DIM, DIM), dtype=jnp.float32) * s(DIM)
        xav = np.sqrt(6.0 / (HEADS + HEAD_DIM))
        u_bias = jax.random.uniform(ks[3], (HEADS, HEAD_DIM), dtype=jnp.float32, minval=-xav, maxval=xav)
        v_bias = jax.random.uniform(ks[4], (HEADS, HEAD_DIM), dtype=jnp.float32, minval=-xav, maxval=xav)
        Wproj = jax.random.normal(ks[5], (DIM, DIM), dtype=jnp.float32) * s(DIM)
        bproj = jax.random.normal(ks[6], (DIM,), dtype=jnp.float32) * 0.01
        return {'x': x, 'Wqkv': Wqkv, 'Wpos': Wpos, 'u_bias': u_bias, 'v_bias': v_bias, 'Wproj': Wproj, 'bproj': bproj}
    _L0_attn_all = _L0_attn_setup()
    _L0_attn_in = {k: v for k, v in _L0_attn_all.items() if k in ('Wqkv', 'Wpos', 'u_bias', 'v_bias', 'Wproj', 'bproj')}
    del _L0_attn_all

    def _L0_ffn_setup():
        import jax, jax.numpy as jnp
        import numpy as np

        def _haar_dwt2(x):
            a = x[:, ::2, ::2]
            b = x[:, ::2, 1::2]
            c = x[:, 1::2, ::2]
            d = x[:, 1::2, 1::2]
            ll = (a + b + c + d) * 0.5
            lh = (a + b - c - d) * 0.5
            hl = (a - b + c - d) * 0.5
            hh = (a - b - c + d) * 0.5
            return (ll, lh, hl, hh)

        def _haar_idwt2(ll, lh, hl, hh):
            a = (ll + lh + hl + hh) * 0.5
            b = (ll + lh - hl - hh) * 0.5
            c = (ll - lh + hl - hh) * 0.5
            d = (ll - lh - hl + hh) * 0.5
            B, H2, W2 = ll.shape
            out = jnp.zeros((B, 2 * H2, 2 * W2), ll.dtype)
            out = out.at[:, ::2, ::2].set(a)
            out = out.at[:, ::2, 1::2].set(b)
            out = out.at[:, 1::2, ::2].set(c)
            out = out.at[:, 1::2, 1::2].set(d)
            return out

        def _interp_linear_last(x, m):
            n = x.shape[-1]
            pos = jnp.linspace(0.0, 1.0, m, dtype=x.dtype) * (n - 1)
            i0 = jnp.clip(jnp.floor(pos).astype(jnp.int32), 0, n - 2)
            w = pos - i0.astype(x.dtype)
            return x[..., i0] * (1.0 - w) + x[..., i0 + 1] * w
        key = jax.random.key(seed)
        k0, k1, k2 = jax.random.split(key, 3)
        b, f, c, hidden = (128, 64, 128, 512)
        x = jax.random.normal(k0, (b, f, c), dtype=jnp.float32)
        fc1_w = jax.random.normal(k1, (hidden, c), dtype=jnp.float32) * 0.02
        fc1_b = jnp.zeros((hidden,), dtype=jnp.float32)
        fc2_w = jax.random.normal(k2, (c // 2, hidden), dtype=jnp.float32) * 0.02
        fc2_b = jnp.zeros((c // 2,), dtype=jnp.float32)
        return {'x': x, 'fc1_w': fc1_w, 'fc1_b': fc1_b, 'fc2_w': fc2_w, 'fc2_b': fc2_b}
    _L0_ffn_all = _L0_ffn_setup()
    _L0_ffn_in = {k: v for k, v in _L0_ffn_all.items() if k in ('fc1_w', 'fc1_b', 'fc2_w', 'fc2_b')}
    del _L0_ffn_all
    return {'x': x, 'x_txt': x_txt, 'L0_tok_w': _L0_tok_in['w'], 'L0_tok_b': _L0_tok_in['b'], 'L0_txt_w': _L0_txt_in['w'], 'L0_attn_Wqkv': _L0_attn_in['Wqkv'], 'L0_attn_Wpos': _L0_attn_in['Wpos'], 'L0_attn_u_bias': _L0_attn_in['u_bias'], 'L0_attn_v_bias': _L0_attn_in['v_bias'], 'L0_attn_Wproj': _L0_attn_in['Wproj'], 'L0_attn_bproj': _L0_attn_in['bproj'], 'L0_ffn_fc1_w': _L0_ffn_in['fc1_w'], 'L0_ffn_fc1_b': _L0_ffn_in['fc1_b'], 'L0_ffn_fc2_w': _L0_ffn_in['fc2_w'], 'L0_ffn_fc2_b': _L0_ffn_in['fc2_b']}

def reference(x, x_txt, L0_tok_w, L0_tok_b, L0_txt_w, L0_attn_Wqkv, L0_attn_Wpos, L0_attn_u_bias, L0_attn_v_bias, L0_attn_Wproj, L0_attn_bproj, L0_ffn_fc1_w, L0_ffn_fc1_b, L0_ffn_fc2_w, L0_ffn_fc2_b):
    import jax
    import jax.numpy as jnp

    def _L0_tok_ref(img, w, b, patch_size):
        import jax, jax.numpy as jnp
        import numpy as np
        B, C, H, W = img.shape
        p = patch_size
        Hp, Wp = (H // p, W // p)
        S = Hp * Wp
        patches = img.reshape(B, C, Hp, p, Wp, p)
        patches = patches.transpose(0, 2, 4, 1, 3, 5).reshape(B, S, C * p * p)
        out = jnp.einsum('bsk,ek->bse', patches, w) + b
        return out

    def _L0_txt_ref(token_ids, w):
        import jax, jax.numpy as jnp
        import numpy as np
        VOCAB = 50257
        D_MODEL = 128
        B, S = (4, 1024)
        return jnp.take(w, token_ids, axis=0)

    def _L0_attn_ref(x, Wqkv, Wpos, u_bias, v_bias, Wproj, bproj):
        import jax, jax.numpy as jnp
        import numpy as np
        DIM = 128
        HEADS = 8
        HEAD_DIM = DIM // HEADS

        def sinusoidal_pe(length, d_model):
            pos = jnp.arange(length, dtype=jnp.float32)[:, None]
            div = jnp.exp(jnp.arange(0, d_model, 2, dtype=jnp.float32) * (-jnp.log(jnp.float32(10000.0)) / d_model))
            ang = pos * div
            return jnp.stack([jnp.sin(ang), jnp.cos(ang)], axis=-1).reshape(length, d_model)

        def relative_shift(pos_score):
            B, H, N, M = pos_score.shape
            padded = jnp.pad(pos_score, ((0, 0), (0, 0), (0, 0), (1, 0)))
            padded = padded.reshape(B, H, M + 1, N)
            return padded[:, :, 1:].reshape(B, H, N, M)
        B, N, C = x.shape
        scale = HEAD_DIM ** (-0.5)
        qkv = (x @ Wqkv).reshape(B, N, 3, HEADS, HEAD_DIM)
        q = qkv[:, :, 0].transpose(0, 2, 1, 3)
        k = qkv[:, :, 1].transpose(0, 2, 1, 3)
        v = qkv[:, :, 2].transpose(0, 2, 1, 3)
        pe = sinusoidal_pe(N, C)
        p = (pe @ Wpos).reshape(N, HEADS, HEAD_DIM)
        content = jnp.einsum('bhnd,bhmd->bhnm', q + u_bias[None, :, None, :], k)
        pos_score = jnp.einsum('bhnd,mhd->bhnm', q + v_bias[None, :, None, :], p)
        pos_score = relative_shift(pos_score)
        attn = jax.nn.softmax((pos_score + content) * scale, axis=-1)
        out = jnp.einsum('bhnm,bhmd->bhnd', attn, v).transpose(0, 2, 1, 3).reshape(B, N, C)
        return out @ Wproj + bproj

    def _L0_ffn_ref(x, fc1_w, fc1_b, fc2_w, fc2_b):
        import jax, jax.numpy as jnp
        import numpy as np

        def _haar_dwt2(x):
            a = x[:, ::2, ::2]
            b = x[:, ::2, 1::2]
            c = x[:, 1::2, ::2]
            d = x[:, 1::2, 1::2]
            ll = (a + b + c + d) * 0.5
            lh = (a + b - c - d) * 0.5
            hl = (a - b + c - d) * 0.5
            hh = (a - b - c + d) * 0.5
            return (ll, lh, hl, hh)

        def _haar_idwt2(ll, lh, hl, hh):
            a = (ll + lh + hl + hh) * 0.5
            b = (ll + lh - hl - hh) * 0.5
            c = (ll - lh + hl - hh) * 0.5
            d = (ll - lh - hl + hh) * 0.5
            B, H2, W2 = ll.shape
            out = jnp.zeros((B, 2 * H2, 2 * W2), ll.dtype)
            out = out.at[:, ::2, ::2].set(a)
            out = out.at[:, ::2, 1::2].set(b)
            out = out.at[:, 1::2, ::2].set(c)
            out = out.at[:, 1::2, 1::2].set(d)
            return out

        def _interp_linear_last(x, m):
            n = x.shape[-1]
            pos = jnp.linspace(0.0, 1.0, m, dtype=x.dtype) * (n - 1)
            i0 = jnp.clip(jnp.floor(pos).astype(jnp.int32), 0, n - 2)
            w = pos - i0.astype(x.dtype)
            return x[..., i0] * (1.0 - w) + x[..., i0 + 1] * w
        b, f, c = x.shape
        ll, lh, hl, hh = _haar_dwt2(x)
        ll_up = _interp_linear_last(ll, c)
        h = jax.nn.gelu(jnp.einsum('bfc,hc->bfh', ll_up, fc1_w) + fc1_b, approximate=False)
        ll_new = jnp.einsum('bfh,oh->bfo', h, fc2_w) + fc2_b
        return _haar_idwt2(ll_new, lh, hl, hh)
    h = _L0_tok_ref(x, L0_tok_w, L0_tok_b, 16)
    h = jnp.concatenate([h, _L0_txt_ref(x_txt, L0_txt_w)], axis=1)
    h = h + _L0_attn_ref(_layernorm(h, axis=-1), L0_attn_Wqkv, L0_attn_Wpos, L0_attn_u_bias, L0_attn_v_bias, L0_attn_Wproj, L0_attn_bproj)
    h = h + _L0_ffn_ref(_layernorm(h, axis=-1), L0_ffn_fc1_w, L0_ffn_fc1_b, L0_ffn_fc2_w, L0_ffn_fc2_b)
    return h

_drawn_inputs = setup_inputs


def setup_inputs(seed=0):
    import zlib

    import numpy as np

    out = dict(_drawn_inputs(seed))
    spreads = {'L0_ffn_fc1_b': (0.0, 0.8), 'L0_ffn_fc2_b': (0.0, 0.284)}
    factors = {'L0_attn_v_bias': 3.536,
     'L0_attn_bproj': 6.121,
     'L0_ffn_fc1_w': 4.712,
     'L0_ffn_fc2_w': 3.995}
    for name, (base, spread) in spreads.items():
        noise = np.random.default_rng([zlib.crc32(name.encode()), seed]).standard_normal(out[name].shape)
        drawn = base * np.exp(spread * noise) if base else spread * noise
        out[name] = jnp.asarray(drawn.astype(out[name].dtype))
    for name, factor in factors.items():
        out[name] = (out[name] * factor).astype(out[name].dtype)
    return out
```

```python
from contextlib import ExitStack

import concourse.bass as bass
from concourse import mybir

F32 = mybir.dt.float32
BF16 = mybir.dt.bfloat16
I32 = mybir.dt.int32
ALU = mybir.AluOpType
ACT = mybir.ActivationFunctionType
AXIS_X = mybir.AxisListType.X

BATCH = 8
CH = 128
HEADS = 8
DH = CH // HEADS
IMG = 196
TXT = 512
SEQ = IMG + TXT
TILES = 6
TP = SEQ // TILES
HALF = SEQ // 2
KP = 6
HID = 512
LOW = CH // 2
EPS = 1e-5
SCALE = DH**-0.5

GROUP = 4
ROWS = 120
STEPS = 6
SLOTS = 6
Q_PARTS = (0, 0, 0, 1, 1, 2)
K_PARTS = (0, 1, 2, 0, 1, 0)
PACKED = SLOTS * DH
VW = 32
UNITS = HEADS // GROUP
SPLIT_QU, SPLIT_QV, SPLIT_K = range(3)


def rows_of(t):
    return min(ROWS, SEQ - t * ROWS)


class Tally:

    def __init__(self, sem, per, before=0):
        self.sem, self.per, self.before, self.n = sem, per, before, 0

    def start(self, it):
        self.base, self.n = it * self.per + self.before, 0

    def inc(self, instruction):
        instruction.then_inc(self.sem, 1)
        self.n += 1
        return self.base + self.n

    def close(self):
        assert self.n == self.per, (self.n, self.per)


def alone(eng):
    eng.nop(nofuse=True)


def tiles3(ap, width):
    return ap[:, :, 0:3 * width].rearrange("p a (b c) -> p a b c", b=3)


def spread(ap, n):
    return ap.unsqueeze(2).broadcast_to([ap.shape[0], ap.shape[1], n])


LN_STEPS = 6


def layernorm_mean(dve, tally, h, total, mean):
    m = tally.inc(dve.reduce_sum(total, h, AXIS_X))
    dve.wait_ge(tally.sem, m)
    return tally.inc(dve.tensor_scalar(mean, total, 1.0 / CH, None, ALU.mult))


def layernorm_center(dve, tally, h, mean, centered, mean_mark):
    dve.wait_ge(tally.sem, mean_mark)
    return dve.tensor_tensor(centered, h, spread(mean, CH), ALU.subtract)


def layernorm_variance(dve, tally, squares, total, var):
    m = tally.inc(dve.reduce_sum(total, squares, AXIS_X))
    dve.wait_ge(tally.sem, m)
    return dve.tensor_scalar(var, total, 1.0 / CH, EPS, ALU.mult, ALU.add)


def prepare(nc, io, dram):
    PAIRS = BATCH // 2
    with ExitStack() as ctx:
        def sb(name, shape, dt=F32):
            return ctx.enter_context(nc.sbuf_tensor("pr_" + name, shape, dt))

        def psum(name, shape, dt=F32):
            return ctx.enter_context(nc.psum_tensor("pr_" + name, shape, dt))

        def sem(name):
            return ctx.enter_context(nc.semaphore("pr_" + name))

        ident = sb("ident", [128, 128])
        tok_w = sb("tok_w", [128, KP, CH])
        w_qkv = sb("w_qkv", [CH, 3 * CH])
        w_pos = sb("w_pos", [CH, CH])
        pe_t = sb("pe_t", [CH, SEQ])
        cols = sb("cols", [CH, 3])
        minus_half = sb("minus_half", [128, TILES])
        patches = [sb(f"patches{i}", [128, KP, IMG]) for i in range(2)]
        index = [sb(f"index{i}", [TP, TILES], I32) for i in range(2)]
        emb_t = [sb(f"emb_t{i}", [CH, IMG]) for i in range(2)]
        h = [sb(f"h{i}", [TP, TILES, CH]) for i in range(2)]
        total = [sb(f"total{i}", [TP, TILES]) for i in range(2)]
        mean = [sb(f"mean{i}", [TP, TILES]) for i in range(2)]
        var = [sb(f"var{i}", [TP, TILES]) for i in range(2)]
        rstd = [sb(f"rstd{i}", [TP, TILES]) for i in range(2)]
        centered = [sb(f"centered{i}", [TP, TILES, CH]) for i in range(2)]
        squares = [sb(f"squares{i}", [TP, TILES, CH]) for i in range(2)]
        normed = [sb(f"normed{i}", [TP, TILES, CH]) for i in range(2)]
        normed_t = [sb(f"normed_t{i}", [CH, SEQ]) for i in range(2)]
        rest = [[sb(f"rest{i}{t}", [CH, SEQ]) for t in range(3)] for i in range(2)]
        parts = [[sb(f"parts{i}{t}", [CH, 3, SEQ], BF16) for t in range(3)] for i in range(2)]
        v_ones = [sb(f"v_ones{i}", [TP, UNITS, TILES, GROUP, VW]) for i in range(2)]

        ps_emb = psum("emb", [128, 2, 512])
        ps_turn = psum("turn", [128, 2, 512])
        ps_proj = psum("proj", [128, 2, 512])
        ps_v = psum("v", [128, 2, 512])

        consts_in = sem("consts_in")
        presets = sem("presets")
        patches_in = [sem(f"patches_in{i}") for i in range(2)]
        index_in = [sem(f"index_in{i}") for i in range(2)]
        gathered = [sem(f"gathered{i}") for i in range(2)]
        embedded = sem("embedded")
        emb_biased = sem("emb_biased")
        emb_turned = sem("emb_turned")
        emb_placed = sem("emb_placed")
        dve_step = sem("dve_step")
        centered_ok = sem("centered_ok")
        squared = sem("squared")
        var_ok = sem("var_ok")
        rstd_ok = sem("rstd_ok")
        normed_ok = sem("normed_ok")
        normed_turned = sem("normed_turned")
        normed_t_ok = sem("normed_t_ok")
        projected = sem("projected")
        v_done = sem("v_done")
        v_placed = sem("v_placed")
        first_part = sem("first_part")
        rest_ok = sem("rest_ok")
        second_part = sem("second_part")
        third_part = sem("third_part")
        h_stored = [sem(f"h_stored{i}") for i in range(2)]
        v_stored = [sem(f"v_stored{i}") for i in range(2)]
        parts_stored = [sem(f"parts_stored{i}") for i in range(2)]
        pos_stored = sem("pos_stored")

        block = ctx.enter_context(nc.Block())

        @block.sync
        def _(sp):
            for dst, src in ((tok_w, io["tok_w"]), (w_qkv, io["w_qkv"]), (w_pos, io["w_pos"]),
                             (pe_t, io["pe_t"]), (cols, io["cols"]), (ident, io["ident"])):
                sp.dma_start(dst[:], src).then_inc(consts_in, 16)
            sp.wait_ge(consts_in, 96)
            with sp.Fori(0, PAIRS) as it:
                for i in range(2):
                    sp.wait_ge(embedded, 2 * it)
                    alone(sp)
                    sp.dma_start(patches[i][:], io["patches"][2 * it + i]).then_inc(patches_in[i], 16)
                for i in range(2):
                    sp.wait_ge(emb_placed, 2 * it + i + 1)
                    alone(sp)
                    sp.wait_ge(gathered[i], 16 * TILES * (it + 1))
                    alone(sp)
                    sp.dma_start(dram["h"][2 * it + i], h[i][:]).then_inc(h_stored[i], 16)
                for i in range(2):
                    sp.wait_ge(v_placed, 2 * it + i + 1)
                    alone(sp)
                    sp.dma_start(dram["v"][2 * it + i].rearrange("g p x -> p g x"),
                                 v_ones[i][:].rearrange("p g j h w -> p g (j h w)")
                                 ).then_inc(v_stored[i], 16)
                for i in range(2):
                    for t in range(3):
                        sp.wait_ge(third_part, 1 + 6 * it + 3 * i + t + 1)
                        alone(sp)
                        sp.dma_start(dram["qk"][2 * it + i, t].rearrange("s c n -> c s n"),
                                     parts[i][t][:]).then_inc(parts_stored[i], 16)
            for i in range(2):
                sp.wait_ge(h_stored[i], 16 * PAIRS)
                sp.wait_ge(v_stored[i], 16 * PAIRS)
                sp.wait_ge(parts_stored[i], 48 * PAIRS)
            sp.wait_ge(pos_stored, 16)

        @block.gpsimd
        def _(pool):
            pool.memset(minus_half[:], -0.5).then_inc(presets, 1)
            for i in range(2):
                pool.memset(v_ones[i][:], 1.0).then_inc(presets, 1)
            pool.wait_ge(presets, 3)
            pool.wait_ge(third_part, 1)
            pool.dma_start(dram["pos"].rearrange("s c n -> c s n"), parts[1][2][:]).then_inc(pos_stored, 16)
            with pool.Fori(0, PAIRS) as it:
                for i in range(2):
                    pool.wait_ge(gathered[i], 16 * TILES * it)
                    pool.dma_start(index[i][:], io["index"][2 * it + i]).then_inc(index_in[i], 16)
                for i in range(2):
                    pool.wait_ge(index_in[i], 16 * (it + 1))
                    pool.wait_ge(centered_ok, 2 * it)
                    pool.wait_ge(h_stored[i], 16 * it)
                    alone(pool)
                    for j in range(TILES):
                        pool.indirect_dma_start(
                            h[i][:, j, :], None, io["table"],
                            bass.IndirectOffsetOnAxis(ap=index[i][:, j:j + 1], axis=0),
                        ).then_inc(gathered[i], 16)
                for i in range(2):
                    pool.wait_ge(presets, 1)
                    pool.wait_ge(var_ok, 2 * it + i + 1)
                    pool.wait_ge(normed_ok, 2 * it)
                    pool.tensor_tensor(rstd[i][:], var[i][:], minus_half[0:TP, :], ALU.pow).then_inc(rstd_ok, 1)

        @block.tensor
        def _(pe):
            pe.wait_ge(consts_in, 96)
            for a in range(2):
                last = pe.matmul(ps_proj[:, a, 0:HALF], w_pos[:], pe_t[:, a * HALF:(a + 1) * HALF],
                                 start=True, stop=True)
            last.then_inc(projected, 1)
            with pe.Fori(0, PAIRS) as it:
                for i in range(2):
                    pe.wait_ge(patches_in[i], 16 * (it + 1))
                    pe.wait_ge(emb_biased, 2 * it)
                    for c in range(KP):
                        last = pe.matmul(ps_emb[:, i, 0:IMG], tok_w[:, c, :], patches[i][:, c, :],
                                         start=(c == 0), stop=(c == KP - 1))
                    last.then_inc(embedded, 1)
                for i in range(2):
                    pe.wait_ge(emb_biased, 2 * it + i + 1)
                    if i == 0:
                        pe.wait_ge(normed_t_ok, 2 * it)
                    else:
                        pe.wait_ge(emb_placed, 2 * it + 1)
                    alone(pe)
                    for j in range(TILES):
                        n = (IMG - j + TILES - 1) // TILES
                        last = pe.transpose(tiles3(ps_turn, CH)[0:n, j // 3, j % 3, :],
                                            emb_t[i][:, j:IMG:TILES], ident[:])
                    last.then_inc(emb_turned, 1)
                for i in range(2):
                    pe.wait_ge(normed_ok, 2 * it + i + 1)
                    if i == 0:
                        pe.wait_ge(emb_placed, 2 * it + 2)
                    else:
                        pe.wait_ge(normed_t_ok, 2 * it + 1)
                    for j in range(TILES):
                        last = pe.transpose(tiles3(ps_turn, TP)[:, j // 3, j % 3, :],
                                            normed[i][:, j, :], ident[0:TP, 0:TP])
                    last.then_inc(normed_turned, 1)
                for i in range(2):
                    pe.wait_ge(normed_t_ok, 2 * it + i + 1)
                    for m in range(2):
                        pe.wait_ge(first_part, 1 + 6 * it + 3 * i + 2 * m)
                        for a in range(2):
                            last = pe.matmul(ps_proj[:, a, 0:HALF], w_qkv[:, m * CH:(m + 1) * CH],
                                             normed_t[i][:, a * HALF:(a + 1) * HALF], start=True, stop=True)
                        last.then_inc(projected, 1)
                    pe.wait_ge(v_placed, 2 * it + i)
                    for j in range(TILES):
                        last = pe.matmul(tiles3(ps_v, CH)[0:TP, j // 3, j % 3, :],
                                         normed_t[i][:, j:SEQ:TILES], w_qkv[:, 2 * CH:3 * CH],
                                         start=True, stop=True)
                    last.then_inc(v_done, 1)

        @block.scalar
        def _(act):
            def halves(tile):
                return tile.rearrange("c (a n) -> c a n", a=2)

            def split_first(x, part, bias):
                src = ps_proj[:, :, 0:HALF]
                act.activation(halves(x[:]), src, ACT.Identity, bias=bias)
                return act.activation(halves(part[:, 0, :]), src, ACT.Identity, bias=bias)

            act.wait_ge(consts_in, 96)
            act.wait_ge(projected, 1)
            split_first(rest[1][2], parts[1][2], 0.0).then_inc(first_part, 1)
            act.wait_ge(rest_ok, 1)
            act.activation(parts[1][2][:, 1, :], rest[1][2][:], ACT.Copy).then_inc(second_part, 1)
            with act.Fori(0, PAIRS) as it:
                for i in range(2):
                    act.wait_ge(embedded, 2 * it + i + 1)
                    act.wait_ge(emb_turned, 2 * it)
                    act.activation(emb_t[i][:], ps_emb[:, i, 0:IMG], ACT.Identity,
                                   bias=cols[:, 0:1]).then_inc(emb_biased, 1)
                for i in range(2):
                    act.wait_ge(centered_ok, 2 * it + i + 1)
                    act.wait_ge(var_ok, 2 * it)
                    act.activation(squares[i][:], centered[i][:], ACT.Square).then_inc(squared, 1)
                for i in range(2):
                    act.wait_ge(normed_turned, 2 * it + i + 1)
                    act.wait_ge(projected, 1 + 4 * it)
                    act.wait_ge(v_done, 2 * it)
                    act.activation(normed_t[i][:].rearrange("c (p a b) -> c a b p", a=2, b=3),
                                   tiles3(ps_turn, TP), ACT.Copy).then_inc(normed_t_ok, 1)
                for i in range(2):
                    act.wait_ge(third_part, 1 + 6 * it)
                    act.wait_ge(parts_stored[i], 48 * it)
                    if i == 1:
                        act.wait_ge(pos_stored, 16)
                    act.wait_ge(projected, 1 + 4 * it + 2 * i + 1)
                    split_first(rest[i][SPLIT_QU], parts[i][SPLIT_QU], cols[:, 1:2]).then_inc(first_part, 1)
                    split_first(rest[i][SPLIT_QV], parts[i][SPLIT_QV], cols[:, 2:3]).then_inc(first_part, 1)
                    act.wait_ge(projected, 1 + 4 * it + 2 * i + 2)
                    split_first(rest[i][SPLIT_K], parts[i][SPLIT_K], 0.0).then_inc(first_part, 1)
                for i in range(2):
                    for t in range(3):
                        act.wait_ge(rest_ok, 1 + 6 * it + 3 * i + t + 1)
                        act.activation(parts[i][t][:, 1, :], rest[i][t][:], ACT.Copy).then_inc(second_part, 1)

        @block.vector
        def _(dve):
            step = Tally(dve_step, 6)
            dve.wait_ge(first_part, 1)
            dve.tensor_tensor(rest[1][2][:], rest[1][2][:], parts[1][2][:, 0, :],
                              ALU.subtract).then_inc(rest_ok, 1)
            dve.wait_ge(second_part, 1)
            dve.tensor_tensor(parts[1][2][:, 2, :], rest[1][2][:], parts[1][2][:, 1, :],
                              ALU.subtract).then_inc(third_part, 1)
            with dve.Fori(0, PAIRS) as it:
                step.start(it)
                for i in range(2):
                    dve.wait_ge(gathered[i], 16 * TILES * (it + 1))
                    dve.wait_ge(emb_turned, 2 * it + i + 1)
                    src = tiles3(ps_turn, CH)
                    dve.tensor_copy(h[i][0:32].rearrange("p (a b) c -> p a b c", a=2), src[0:32])
                    dve.tensor_copy(h[i][32:33, 0:3, :], src[32:33, 0, :, :])
                    dve.tensor_copy(h[i][32:33, 3:4, :], src[32:33, 1, 0:1, :]).then_inc(emb_placed, 1)
                means = []
                for i in range(2):
                    dve.wait_ge(emb_placed, 2 * it + i + 1)
                    means.append(layernorm_mean(dve, step, h[i][:], total[i][:], mean[i][:]))
                for i in range(2):
                    dve.wait_ge(squared, 2 * it)
                    layernorm_center(dve, step, h[i][:], mean[i][:], centered[i][:],
                                     means[i]).then_inc(centered_ok, 1)
                for i in range(2):
                    dve.wait_ge(squared, 2 * it + i + 1)
                    dve.wait_ge(rstd_ok, 2 * it)
                    layernorm_variance(dve, step, squares[i][:], total[i][:], var[i][:]).then_inc(var_ok, 1)
                step.close()
                for i in range(2):
                    dve.wait_ge(rstd_ok, 2 * it + i + 1)
                    dve.wait_ge(normed_turned, 2 * it)
                    dve.tensor_tensor(normed[i][:], centered[i][:], spread(rstd[i][:], CH),
                                      ALU.mult).then_inc(normed_ok, 1)
                for i in range(2):
                    dve.wait_ge(presets, 3)
                    dve.wait_ge(v_done, 2 * it + i + 1)
                    dve.wait_ge(v_stored[i], 16 * it)
                    for g in range(UNITS):
                        last = dve.tensor_copy(
                            v_ones[i][:, g, :, :, 0:DH].rearrange("p (a b) h d -> p a b h d", a=2),
                            tiles3(ps_v, CH)[0:TP, :, :, g * GROUP * DH:(g + 1) * GROUP * DH]
                            .rearrange("p a b (h d) -> p a b h d", h=GROUP))
                    last.then_inc(v_placed, 1)
                for i in range(2):
                    for t in range(3):
                        dve.wait_ge(first_part, 1 + 6 * it + 3 * i + t + 1)
                        dve.tensor_tensor(rest[i][t][:], rest[i][t][:], parts[i][t][:, 0, :],
                                          ALU.subtract).then_inc(rest_ok, 1)
                for i in range(2):
                    for t in range(3):
                        dve.wait_ge(second_part, 1 + 6 * it + 3 * i + t + 1)
                        dve.tensor_tensor(parts[i][t][:, 2, :], rest[i][t][:], parts[i][t][:, 1, :],
                                          ALU.subtract).then_inc(third_part, 1)


def attend(nc, dram):
    SLOTS_U = STEPS * GROUP
    SLOTS_B = UNITS * SLOTS_U
    STEPS_B = UNITS * STEPS
    THIRD = 2 * GROUP
    THIRDS_U = SLOTS_U // THIRD
    THIRDS_B = UNITS * THIRDS_U
    LAG = 2
    PV_FROM = 2
    COLS = 2 * ROWS
    Y_RING = 3

    with ExitStack() as ctx:
        def sb(name, shape, dt=F32):
            return ctx.enter_context(nc.sbuf_tensor("at_" + name, shape, dt))

        def psum(name, shape, dt=F32):
            return ctx.enter_context(nc.psum_tensor("at_" + name, shape, dt))

        def sem(name):
            return ctx.enter_context(nc.semaphore("at_" + name))

        ident = sb("ident", [128, 128])
        pos_pack = sb("pos_pack", [PACKED, HEADS, SEQ], BF16)
        qv_pack = [sb(f"qv_pack{g}", [PACKED, GROUP, SEQ], BF16) for g in range(UNITS)]
        qu_pack = [sb(f"qu_pack{g}", [PACKED, GROUP, SEQ], BF16) for g in range(UNITS)]
        k_pack = [sb(f"k_pack{g}", [PACKED, GROUP, SEQ], BF16) for g in range(UNITS)]
        v_ones = [sb(f"v_ones{g}", [TP, TILES, GROUP, VW]) for g in range(UNITS)]
        raw = [sb(f"raw{i}", [ROWS, GROUP, SEQ + 1]) for i in range(2)]
        shifted = [sb(f"shifted{i}", [ROWS, GROUP, SEQ]) for i in range(Y_RING)]
        top = sb("top", [ROWS, 4])
        probs_t = [sb(f"probs_t{i}", [TP, GROUP, TILES, COLS]) for i in range(2)]
        out_t = [sb(f"out_t{g}", [128, SEQ]) for g in range(UNITS)]

        ps_pos = psum("pos", [128, 2, 512])
        ps_key = psum("key", [128, 2, 512])
        ps_turn = psum("turn", [128, 2, 512])
        ps_out = psum("out", [128, 512])

        consts_in = sem("consts_in")
        pos_in = sem("pos_in")
        zero_front = sem("zero_front")
        qv_in = [sem(f"qv_in{g}") for g in range(UNITS)]
        qk_in = [sem(f"qk_in{g}") for g in range(UNITS)]
        v_in = [sem(f"v_in{g}") for g in range(UNITS)]
        pos_scored = sem("pos_scored")
        pos_read = sem("pos_read")
        raw_stored = [sem(f"raw_stored{i}") for i in range(2)]
        shifted_in = [sem(f"shifted_in{i}") for i in range(Y_RING)]
        key_scored = sem("key_scored")
        summed = sem("summed")
        lowered = sem("lowered")
        turned = sem("turned")
        expd = sem("expd")
        weighed = sem("weighed")
        out_read = sem("out_read")
        out_stored = [sem(f"out_stored{g}") for g in range(UNITS)]

        def count(b, per, n):
            value = b * per + n
            return None if isinstance(value, int) and value <= 0 else value

        def wait(eng, sem, value):
            if value is not None:
                eng.wait_ge(sem, value)

        def unit_exists(b, u):
            return not isinstance(b, int) or 0 <= b * UNITS + u < BATCH * UNITS

        block = ctx.enter_context(nc.Block())

        def store_raw(sp, b, k):
            g, t = k // STEPS % UNITS, k % STEPS
            wait(sp, pos_read, count(b, SLOTS_B, GROUP * (k + 1)))
            alone(sp)
            rows = dram["raw"][g].rearrange("h (n w) -> n h w", w=SEQ + 1)
            sp.dma_start(rows[t * ROWS:t * ROWS + rows_of(t)], raw[k % 2][0:rows_of(t)]
                         ).then_inc(raw_stored[k % 2], 16)

        def load_shifted(sp, b, k):
            g, t = k // STEPS % UNITS, k % STEPS
            wait(sp, turned, count(b, SLOTS_B, GROUP * (k - Y_RING + 1)))
            alone(sp)
            written = k + (1 if t < STEPS - 1 else 0)
            for w in (written, written - 1):
                wait(sp, raw_stored[w % 2], count(b, 8 * STEPS_B, 16 * (w // 2 + 1)))
            alone(sp)
            rows = dram["raw"][g, :, SEQ:SEQ * (SEQ + 1)].rearrange("h (n m) -> n h m", m=SEQ)
            sp.dma_start(shifted[k % Y_RING][0:rows_of(t)], rows[t * ROWS:t * ROWS + rows_of(t)]
                         ).then_inc(shifted_in[k % Y_RING], 16)

        @block.sync
        def _(sp):
            sp.dma_start(ident[:], dram["ident"]).then_inc(consts_in, 16)
            for k in range(STEPS):
                store_raw(sp, 0, k)
            for k in range(Y_RING - 1):
                load_shifted(sp, 0, k)

            def batch(b):
                for k in range(STEPS_B):
                    if unit_exists(b, (k + Y_RING - 1) // STEPS):
                        load_shifted(sp, b, k + Y_RING - 1)
                    if unit_exists(b, k // STEPS + 1):
                        store_raw(sp, b, k + STEPS)

            batch(0)
            with sp.Fori(1, BATCH - 1) as b:
                batch(b)
            batch(BATCH - 1)

        @block.gpsimd
        def _(pool):
            def load_pack(dst, src, parts, g, arrived):
                for s, part in enumerate(parts):
                    heads = src[part, g * GROUP * DH:(g + 1) * GROUP * DH].rearrange("(h d) n -> d h n", d=DH)
                    pool.dma_start(dst[s * DH:(s + 1) * DH], heads).then_inc(arrived, 16)

            def load_qv(b, u):
                g = u % UNITS
                wait(pool, pos_scored, count(b, SLOTS_B, SLOTS_U * (u - 1)))
                load_pack(qv_pack[g], dram["qk"][b + u // UNITS, SPLIT_QV], Q_PARTS, g, qv_in[g])

            def load_qk(b, u):
                g = u % UNITS
                wait(pool, key_scored, count(b, SLOTS_B, SLOTS_U * (u - 1)))
                load_pack(qu_pack[g], dram["qk"][b + u // UNITS, SPLIT_QU], Q_PARTS, g, qk_in[g])
                load_pack(k_pack[g], dram["qk"][b + u // UNITS, SPLIT_K], K_PARTS, g, qk_in[g])
                wait(pool, weighed, count(b, THIRDS_B, THIRDS_U * (u - 1)))
                pool.dma_start(v_ones[g][:].rearrange("p j h w -> p (j h w)"),
                               dram["v"][b + u // UNITS, g]).then_inc(v_in[g], 16)

            def store_out(b, u):
                g = u % UNITS
                wait(pool, out_read, count(b, THIRDS_B, THIRDS_U * (u + 1)))
                pool.dma_start(dram["out_t"][b + u // UNITS, g], out_t[g][:]).then_inc(out_stored[g], 16)

            for i in range(2):
                pool.memset(raw[i][:, :, 0:1], 0.0).then_inc(zero_front, 1)
            for s, part in enumerate(K_PARTS):
                src = dram["pos"][part].rearrange("(h d) n -> d h n", d=DH)
                pool.dma_start(pos_pack[s * DH:(s + 1) * DH], src).then_inc(pos_in, 16)
            load_qv(0, 0)
            load_qv(0, 1)
            load_qk(0, 0)

            def batch(b):
                for u in range(UNITS):
                    if unit_exists(b, u + 1):
                        load_qk(b, u + 1)
                    if unit_exists(b, u + 2):
                        load_qv_after(b, u + 2)
                    if unit_exists(b, u - 1):
                        store_out_before(b, u - 1)

            def load_qv_after(b, u):
                g = u % UNITS
                wait(pool, pos_scored, count(b, SLOTS_B, SLOTS_U * (u - 1)))
                load_pack(qv_pack[g], dram["qk"][b + u // UNITS, SPLIT_QV], Q_PARTS, g, qv_in[g])

            def store_out_before(b, u):
                g = u % UNITS
                wait(pool, out_read, count(b, THIRDS_B, THIRDS_U * (u + 1)))
                pool.dma_start(dram["out_t"][b + u // UNITS, g], out_t[g][:]).then_inc(out_stored[g], 16)

            batch(0)
            with pool.Fori(1, BATCH - 1) as b:
                batch(b)
            batch(BATCH - 1)
            store_out(BATCH - 1, UNITS - 1)
            for g in range(UNITS):
                pool.wait_ge(out_stored[g], 16 * BATCH)

        @block.tensor
        def _(pe):
            def score_positions(b, n):
                g, t, hh = n // SLOTS_U % UNITS, n // GROUP % STEPS, n % GROUP
                if t == 0 and hh == 0:
                    wait(pe, qv_in[g], count(b, 16 * SLOTS, 16 * SLOTS * (n // SLOTS_B + 1)))
                wait(pe, pos_read, count(b, SLOTS_B, n))
                rows = rows_of(t)
                for a in range(2):
                    last = pe.matmul(ps_pos[0:rows, a, 0:HALF], qv_pack[g][:, hh, t * ROWS:t * ROWS + rows],
                                     pos_pack[:, g * GROUP + hh, a * HALF:(a + 1) * HALF], start=True, stop=True)
                last.then_inc(pos_scored, 1)

            def score_keys(b, n):
                g, t, hh = n // SLOTS_U, n // GROUP % STEPS, n % GROUP
                if t == 0 and hh == 0:
                    wait(pe, qk_in[g], count(b, 32 * SLOTS, 32 * SLOTS))
                wait(pe, summed, count(b, SLOTS_B, n))
                rows = rows_of(t)
                for a in range(2):
                    last = pe.matmul(ps_key[0:rows, a, 0:HALF], qu_pack[g][:, hh, t * ROWS:t * ROWS + rows],
                                     k_pack[g][:, hh, a * HALF:(a + 1) * HALF], start=True, stop=True)
                last.then_inc(key_scored, 1)

            def turn(b, n):
                t, hh = n // GROUP % STEPS, n % GROUP
                rows = rows_of(t)
                wait(pe, lowered, count(b, SLOTS_B, n + 1))
                wait(pe, expd, count(b, SLOTS_B, n))
                for j in range(TILES):
                    last = pe.transpose(tiles3(ps_turn, ROWS)[0:TP, j // 3, j % 3, 0:rows],
                                        shifted[n // GROUP % Y_RING][0:rows, hh, j:SEQ:TILES],
                                        ident[0:rows, 0:rows])
                last.then_inc(turned, 1)

            def weigh(b, m, j):
                g = m // THIRDS_U % UNITS
                cols = rows_of(m * 2 % STEPS) + rows_of(m * 2 % STEPS + 1)
                if j == 0:
                    wait(pe, expd, count(b, SLOTS_B, THIRD * (m + 1)))
                    wait(pe, out_read, count(b, THIRDS_B, m))
                    wait(pe, v_in[g], count(b, 16, 16 * (m // THIRDS_B + 1)))
                for hh in range(GROUP):
                    last = pe.matmul(ps_out[hh * VW:(hh + 1) * VW, 0:cols], v_ones[g][:, j, hh, :],
                                     probs_t[m % 2][:, hh, j, 0:cols], start=(j == 0), stop=(j == TILES - 1))
                if j == TILES - 1:
                    last.then_inc(weighed, 1)

            def tail(b, n):
                if slot_exists(b, n - LAG):
                    turn(b, n - LAG)
                j = n % THIRD - PV_FROM
                if 0 <= j < TILES and slot_exists(b, n - THIRD):
                    weigh(b, n // THIRD - 1, j)

            def slot_exists(b, n):
                return not isinstance(b, int) or 0 <= b * SLOTS_B + n < BATCH * SLOTS_B

            def batch(b):
                for n in range(SLOTS_B):
                    if unit_exists(b, n // SLOTS_U + 1):
                        score_positions(b, n + SLOTS_U)
                    score_keys(b, n)
                    tail(b, n)

            pe.wait_ge(consts_in, 16)
            pe.wait_ge(pos_in, 16 * SLOTS)
            for n in range(SLOTS_U):
                score_positions(0, n)
            batch(0)
            with pe.Fori(1, BATCH - 1) as b:
                batch(b)
            batch(BATCH - 1)
            for n in range(SLOTS_B, SLOTS_B + THIRD):
                tail(BATCH - 1, n)

        @block.scalar
        def _(act):
            def read_positions(b, n):
                k, t, hh = n // GROUP, n // GROUP % STEPS, n % GROUP
                if hh == 0:
                    wait(act, raw_stored[k % 2], count(b, 8 * STEPS_B, 16 * (k // 2)))
                wait(act, pos_scored, count(b, SLOTS_B, n + 1))
                rows = rows_of(t)
                act.activation(raw[k % 2][0:rows, hh, 1:SEQ + 1].rearrange("p (a n) -> p a n", a=2),
                               ps_pos[0:rows, :, 0:HALF], ACT.Copy).then_inc(pos_read, 1)

            def exponentials(b, n):
                m, t, hh = n // THIRD, n // GROUP % STEPS, n % GROUP
                rows = rows_of(t)
                wait(act, turned, count(b, SLOTS_B, n + 1))
                if n % THIRD == 0:
                    wait(act, weighed, count(b, THIRDS_B, m - 1))
                at = t % 2 * ROWS
                act.activation(probs_t[m % 2][:, hh, :, at:at + rows].rearrange("p (a b) n -> p a b n", a=2),
                               tiles3(ps_turn, ROWS)[0:TP, :, :, 0:rows], ACT.Exp, scale=SCALE).then_inc(expd, 1)

            def read_out(b, m):
                g, k = m // THIRDS_U % UNITS, m * 2 % STEPS
                cols = rows_of(k) + rows_of(k + 1)
                wait(act, weighed, count(b, THIRDS_B, m + 1))
                if k == 0:
                    wait(act, out_stored[g], count(b, 16, 16 * (m // THIRDS_B)))
                act.activation(out_t[g][:, k * ROWS:k * ROWS + cols], ps_out[:, 0:cols],
                               ACT.Copy).then_inc(out_read, 1)

            def tail(b, n):
                if slot_exists(b, n - LAG):
                    exponentials(b, n - LAG)
                if n % THIRD == 0 and slot_exists(b, n - 2 * THIRD):
                    read_out(b, n // THIRD - 2)

            def slot_exists(b, n):
                return not isinstance(b, int) or 0 <= b * SLOTS_B + n < BATCH * SLOTS_B

            def batch(b):
                for n in range(SLOTS_B):
                    if unit_exists(b, n // SLOTS_U + 1):
                        read_positions(b, n + SLOTS_U)
                    tail(b, n)

            act.wait_ge(zero_front, 2)
            for n in range(SLOTS_U):
                read_positions(0, n)
            batch(0)
            with act.Fori(1, BATCH - 1) as b:
                batch(b)
            batch(BATCH - 1)
            for n in range(SLOTS_B, SLOTS_B + THIRD + 1):
                tail(BATCH - 1, n)

        @block.vector
        def _(dve):
            def sum_and_lower(b, n):
                k, t, hh = n // GROUP, n // GROUP % STEPS, n % GROUP
                rows, tile = rows_of(t), shifted[k % Y_RING]
                if hh == 0:
                    wait(dve, shifted_in[k % Y_RING], count(b, 16 * STEPS_B // Y_RING, 16 * (k // Y_RING + 1)))
                wait(dve, key_scored, count(b, SLOTS_B, n + 1))
                alone(dve)
                both = tile[0:rows, hh, :].rearrange("p (a n) -> p a n", a=2)
                dve.tensor_tensor_reduce(out=both, in0=ps_key[0:rows, :, 0:HALF], in1=both, scale=1.0,
                                         scalar=-3.0e38, op0=ALU.add, op1=ALU.max,
                                         accum_out=top[0:rows, hh:hh + 1]).then_inc(summed, 1)
                wait(dve, summed, count(b, SLOTS_B, n + 1))
                dve.tensor_scalar(tile[0:rows, hh, :], tile[0:rows, hh, :], top[0:rows, hh:hh + 1], None,
                                  ALU.subtract).then_inc(lowered, 1)

            def batch(b):
                for n in range(SLOTS_B):
                    sum_and_lower(b, n)

            batch(0)
            with dve.Fori(1, BATCH - 1) as b:
                batch(b)
            batch(BATCH - 1)


def finish(nc, io, dram, out):
    PAIRS = BATCH // 2
    LOWS = TILES // 2
    CHUNKS = HID // 128
    with ExitStack() as ctx:
        def sb(name, shape, dt=F32):
            return ctx.enter_context(nc.sbuf_tensor("fi_" + name, shape, dt))

        def psum(name, shape, dt=F32):
            return ctx.enter_context(nc.psum_tensor("fi_" + name, shape, dt))

        def sem(name):
            return ctx.enter_context(nc.semaphore("fi_" + name))

        ident = sb("ident", [128, 128])
        w_proj = sb("w_proj", [CH, CH])
        b_proj = sb("b_proj", [TP, CH])
        interp_t = sb("interp_t", [CH, LOW])
        fc1_t = sb("fc1_t", [CH, HID])
        fc1_b = sb("fc1_b", [128, CHUNKS])
        fc2_t = sb("fc2_t", [128, CHUNKS, LOW])
        fc2_b = sb("fc2_b", [TP, LOW])
        w_up = sb("w_up", [LOW, HID])
        minus_half = sb("minus_half", [128, TILES])
        heads_t = [sb(f"heads_t{i}", [128, UNITS, SEQ]) for i in range(2)]
        h = [sb(f"h{i}", [TP, TILES, CH]) for i in range(2)]
        inv = [sb(f"inv{i}", [TP, TILES * HEADS]) for i in range(2)]
        heads = [sb(f"heads{i}", [TP, TILES, CH]) for i in range(2)]
        heads_n = [sb(f"heads_n{i}", [CH, TILES, TP]) for i in range(2)]
        total = [sb(f"total{i}", [TP, TILES]) for i in range(2)]
        mean = [sb(f"mean{i}", [TP, TILES]) for i in range(2)]
        var = [sb(f"var{i}", [TP, TILES]) for i in range(2)]
        rstd = [sb(f"rstd{i}", [TP, TILES]) for i in range(2)]
        centered = [sb(f"centered{i}", [TP, TILES, CH]) for i in range(2)]
        squares = [sb(f"squares{i}", [TP, TILES, CH]) for i in range(2)]
        normed = [sb(f"normed{i}", [TP, TILES, CH]) for i in range(2)]
        pairs = [sb(f"pairs{i}", [TP, LOWS, CH]) for i in range(2)]
        low = [sb(f"low{i}", [TP, LOWS, LOW]) for i in range(2)]
        low_t = [sb(f"low_t{i}", [LOW, LOWS * TP]) for i in range(2)]
        hidden = [sb(f"hidden{i}", [128, CHUNKS, LOWS * TP]) for i in range(2)]
        delta = [sb(f"delta{i}", [TP, LOWS, LOW]) for i in range(2)]
        result = [sb(f"result{i}", [TP, TILES, CH]) for i in range(2)]

        ps_heads = psum("heads", [128, 3, 512])
        ps_turn = psum("turn", [128, 2, 512])
        ps_wide = psum("wide", [128, 2, 512])
        ps_low = psum("low", [128, 512])

        consts_in = sem("consts_in")
        exponent = sem("exponent")
        up_done = sem("up_done")
        up_ok = sem("up_ok")
        heads_in = [sem(f"heads_in{i}") for i in range(2)]
        h_in = [sem(f"h_in{i}") for i in range(2)]
        heads_turned = sem("heads_turned")
        dve_step = sem("dve_step")
        heads_ok = sem("heads_ok")
        heads_back = sem("heads_back")
        heads_n_ok = sem("heads_n_ok")
        projected = sem("projected")
        proj_added = sem("proj_added")
        centered_ok = sem("centered_ok")
        squared = sem("squared")
        var_ok = sem("var_ok")
        rstd_ok = sem("rstd_ok")
        low_ok = sem("low_ok")
        low_turned = sem("low_turned")
        low_t_ok = sem("low_t_ok")
        widened = sem("widened")
        activated = sem("activated")
        narrowed = sem("narrowed")
        result_ok = sem("result_ok")
        stored = [sem(f"stored{i}") for i in range(2)]

        block = ctx.enter_context(nc.Block())

        @block.sync
        def _(sp):
            for dst, name in ((w_proj, "w_proj"), (interp_t, "interp_t"), (fc1_t, "fc1_t"), (fc1_b, "fc1_b"),
                              (fc2_t, "fc2_t"), (ident, "ident")):
                sp.dma_start(dst[:], io[name]).then_inc(consts_in, 16)
            sp.dma_start(b_proj[:], io["b_proj"].partition_broadcast(TP)).then_inc(consts_in, 16)
            sp.dma_start(fc2_b[:], io["fc2_b"].partition_broadcast(TP)).then_inc(consts_in, 16)
            sp.wait_ge(consts_in, 128)
            with sp.Fori(0, PAIRS) as it:
                for i in range(2):
                    sp.wait_ge(heads_turned, 2 * it)
                    alone(sp)
                    sp.dma_start(heads_t[i][:], dram["out_t"][2 * it + i].rearrange("g c n -> c g n")
                                 ).then_inc(heads_in[i], 16)
                    sp.wait_ge(result_ok, 2 * it)
                    alone(sp)
                    sp.dma_start(h[i][:], dram["h"][2 * it + i]).then_inc(h_in[i], 16)
                for i in range(2):
                    sp.wait_ge(result_ok, 2 * it + i + 1)
                    alone(sp)
                    sp.dma_start(out[2 * it + i].rearrange("(p j) c -> p j c", j=TILES), result[i][:]
                                 ).then_inc(stored[i], 16)
            for i in range(2):
                sp.wait_ge(stored[i], 16 * PAIRS)

        @block.gpsimd
        def _(pool):
            pool.memset(minus_half[:], -0.5).then_inc(exponent, 1)
            pool.wait_ge(exponent, 1)
            with pool.Fori(0, PAIRS) as it:
                for i in range(2):
                    pool.wait_ge(var_ok, 2 * it + i + 1)
                    pool.wait_ge(low_ok, 2 * it)
                    pool.tensor_tensor(rstd[i][:], var[i][:], minus_half[0:TP, :], ALU.pow).then_inc(rstd_ok, 1)

        @block.tensor
        def _(pe):
            pe.wait_ge(consts_in, 128)
            pe.matmul(ps_wide[0:LOW, 0, :], interp_t[:], fc1_t[:], start=True, stop=True).then_inc(up_done, 1)
            pe.wait_ge(up_ok, 1)
            with pe.Fori(0, PAIRS) as it:
                for i in range(2):
                    pe.wait_ge(heads_in[i], 16 * (it + 1))
                    pe.wait_ge(heads_ok, 2 * it + i)
                    for j in range(TILES):
                        for g in range(UNITS):
                            at = (j % 2 * UNITS + g) * 128
                            last = pe.transpose(ps_heads[0:TP, j // 2, at:at + 128],
                                                heads_t[i][:, g, j:SEQ:TILES], ident[:])
                    last.then_inc(heads_turned, 1)
                for i in range(2):
                    pe.wait_ge(heads_ok, 2 * it + i + 1)
                    if i == 0:
                        pe.wait_ge(low_t_ok, 2 * it)
                    else:
                        pe.wait_ge(heads_n_ok, 2 * it + 1)
                    for j in range(TILES):
                        last = pe.transpose(tiles3(ps_turn, TP)[:, j // 3, j % 3, :], heads[i][:, j, :],
                                            ident[0:TP, 0:TP])
                    last.then_inc(heads_back, 1)
                for i in range(2):
                    pe.wait_ge(heads_n_ok, 2 * it + i + 1)
                    if i == 0:
                        pe.wait_ge(activated, 2 * CHUNKS * it)
                    else:
                        pe.wait_ge(proj_added, 2 * it + 1)
                    for j in range(TILES):
                        last = pe.matmul(tiles3(ps_wide, CH)[0:TP, j // 3, j % 3, :], heads_n[i][:, j, :],
                                         w_proj[:], start=True, stop=True)
                    last.then_inc(projected, 1)
                for i in range(2):
                    pe.wait_ge(low_ok, 2 * it + i + 1)
                    if i == 0:
                        pe.wait_ge(heads_n_ok, 2 * it + 2)
                    else:
                        pe.wait_ge(low_t_ok, 2 * it + 1)
                    alone(pe)
                    for s in range(LOWS):
                        last = pe.transpose(ps_turn[0:LOW, 0, s * TP:(s + 1) * TP], low[i][:, s, :],
                                            ident[0:TP, 0:TP])
                    last.then_inc(low_turned, 1)
                for i in range(2):
                    pe.wait_ge(low_t_ok, 2 * it + i + 1)
                    for c in range(CHUNKS):
                        if i == 0 and c < 2:
                            pe.wait_ge(proj_added, 2 * it + 2)
                        else:
                            pe.wait_ge(activated, 2 * CHUNKS * it + CHUNKS * i + c - 1)
                        pe.matmul(ps_wide[:, c % 2, 0:LOWS * TP], w_up[:, c * 128:(c + 1) * 128], low_t[i][:],
                                  start=True, stop=True).then_inc(widened, 1)
                for i in range(2):
                    pe.wait_ge(activated, 2 * CHUNKS * it + CHUNKS * (i + 1))
                    pe.wait_ge(result_ok, 2 * it + i)
                    for s in range(LOWS):
                        for c in range(CHUNKS):
                            last = pe.matmul(ps_low[0:TP, s * LOW:(s + 1) * LOW],
                                             hidden[i][:, c, s * TP:(s + 1) * TP], fc2_t[:, c, :],
                                             start=(c == 0), stop=(c == CHUNKS - 1))
                    last.then_inc(narrowed, 1)

        @block.scalar
        def _(act):
            act.wait_ge(up_done, 1)
            act.activation(w_up[:], ps_wide[0:LOW, 0, :], ACT.Copy, scale=0.5).then_inc(up_ok, 1)
            with act.Fori(0, PAIRS) as it:
                for i in range(2):
                    act.wait_ge(heads_back, 2 * it + i + 1)
                    act.wait_ge(projected, 2 * it)
                    act.activation(heads_n[i][:].rearrange("c (a b) p -> c a b p", a=2), tiles3(ps_turn, TP),
                                   ACT.Copy).then_inc(heads_n_ok, 1)
                for i in range(2):
                    act.wait_ge(centered_ok, 2 * it + i + 1)
                    act.wait_ge(var_ok, 2 * it)
                    act.activation(squares[i][:], centered[i][:], ACT.Square).then_inc(squared, 1)
                for i in range(2):
                    act.wait_ge(low_turned, 2 * it + i + 1)
                    act.wait_ge(widened, 2 * CHUNKS * it)
                    act.activation(low_t[i][:], ps_turn[0:LOW, 0, 0:LOWS * TP], ACT.Copy).then_inc(low_t_ok, 1)
                for i in range(2):
                    act.wait_ge(narrowed, 2 * it)
                    for c in range(CHUNKS):
                        act.wait_ge(widened, 2 * CHUNKS * it + CHUNKS * i + c + 1)
                        act.activation(hidden[i][:, c, :], ps_wide[:, c % 2, 0:LOWS * TP], ACT.Gelu,
                                       bias=fc1_b[:, c:c + 1]).then_inc(activated, 1)

        @block.vector
        def _(dve):
            step = Tally(dve_step, 20)
            dve.wait_ge(consts_in, 128)
            with dve.Fori(0, PAIRS) as it:
                step.start(it)
                for i in range(2):
                    dve.wait_ge(heads_turned, 2 * it + i + 1)
                    dve.wait_ge(heads_back, 2 * it)
                    src = ps_heads[0:TP].rearrange("p a (x w) -> p (a x) w", w=VW)
                    m = step.inc(dve.reciprocal(inv[i][:], src[:, :, DH]))
                    dve.wait_ge(dve_step, m)
                    dve.tensor_tensor(heads[i][:].rearrange("p j (x d) -> p (j x) d", d=DH), src[:, :, 0:DH],
                                      spread(inv[i][:], DH), ALU.mult).then_inc(heads_ok, 1)
                marks = []
                for i in range(2):
                    dve.wait_ge(h_in[i], 16 * (it + 1))
                    dve.wait_ge(projected, 2 * it + i + 1)
                    h4 = h[i][:].rearrange("p (a b) c -> p a b c", a=2)
                    dve.tensor_tensor(h4, h4, tiles3(ps_wide, CH)[0:TP], ALU.add).then_inc(proj_added, 1)
                for i in range(2):
                    dve.wait_ge(proj_added, 2 * it + i + 1)
                    bias = b_proj[:].unsqueeze(1).broadcast_to([TP, TILES, CH])
                    marks.append(step.inc(dve.tensor_tensor(h[i][:], h[i][:], bias, ALU.add)))
                for i in range(2):
                    dve.wait_ge(dve_step, marks[i])
                    marks[i] = layernorm_mean(dve, step, h[i][:], total[i][:], mean[i][:])
                for i in range(2):
                    layernorm_center(dve, step, h[i][:], mean[i][:], centered[i][:],
                                     marks[i]).then_inc(centered_ok, 1)
                for i in range(2):
                    dve.wait_ge(squared, 2 * it + i + 1)
                    dve.wait_ge(rstd_ok, 2 * it)
                    layernorm_variance(dve, step, squares[i][:], total[i][:], var[i][:]).then_inc(var_ok, 1)
                for i in range(2):
                    dve.wait_ge(rstd_ok, 2 * it + i + 1)
                    marks[i] = step.inc(dve.tensor_tensor(normed[i][:], centered[i][:],
                                                          spread(rstd[i][:], CH), ALU.mult))
                for i in range(2):
                    dve.wait_ge(dve_step, marks[i])
                    y = normed[i][:].rearrange("p (s r) c -> p s r c", r=2)
                    marks[i] = step.inc(dve.tensor_tensor(pairs[i][:], y[:, :, 0, :], y[:, :, 1, :], ALU.add))
                for i in range(2):
                    dve.wait_ge(dve_step, marks[i])
                    dve.wait_ge(low_turned, 2 * it)
                    z = pairs[i][:].rearrange("p s (c e) -> p s c e", e=2)
                    dve.tensor_tensor(low[i][:], z[:, :, :, 0], z[:, :, :, 1], ALU.add).then_inc(low_ok, 1)
                for i in range(2):
                    marks[i] = step.inc(dve.tensor_tensor(h[i][:], h[i][:], normed[i][:], ALU.add))
                for i in range(2):
                    dve.wait_ge(narrowed, 2 * it + i + 1)
                    bias = fc2_b[:].unsqueeze(1).broadcast_to([TP, LOWS, LOW])
                    m = step.inc(dve.tensor_tensor(
                        delta[i][:], ps_low[0:TP, 0:LOWS * LOW].rearrange("p (s c) -> p s c", s=LOWS), bias,
                        ALU.add))
                    dve.wait_ge(dve_step, m)
                    dve.wait_ge(low_ok, 2 * it + i + 1)
                    m = step.inc(dve.scalar_tensor_tensor(out=delta[i][:], in0=low[i][:], scalar=-0.5,
                                                          in1=delta[i][:], op0=ALU.mult, op1=ALU.add))
                    dve.wait_ge(dve_step, m)
                    dve.wait_ge(stored[i], 16 * it)
                    d = delta[i][:].rearrange("p s c -> p (s c)")
                    for r in range(2):
                        def quads(tile):
                            rows = tile[:].rearrange("p (s r) c -> p s r c", r=2)[:, :, r, :]
                            return rows.rearrange("p s (c e) -> p s c e", e=2)
                        change = delta[i][:].unsqueeze(3).broadcast_to([TP, LOWS, LOW, 2])
                        last = dve.scalar_tensor_tensor(out=quads(result[i]), in0=change, scalar=0.5,
                                                        in1=quads(h[i]), op0=ALU.mult, op1=ALU.add)
                    last.then_inc(result_ok, 1)
                step.close()


def layer(nc, io, out):
    dram = {name: nc.dram_tensor("scratch_" + name, shape, dt, kind="Internal").ap() for name, shape, dt in (
        ("h", (BATCH, TP, TILES * CH), F32),
        ("qk", (BATCH, 3, 3, CH, SEQ), BF16),
        ("pos", (3, CH, SEQ), BF16),
        ("v", (BATCH, UNITS, TP, TILES * GROUP * VW), F32),
        ("raw", (UNITS, GROUP, SEQ * (SEQ + 1)), F32),
        ("out_t", (BATCH, UNITS, 128, SEQ), F32),
    )}
    dram["ident"] = io["ident"]
    prepare(nc, io, dram)
    attend(nc, dram)
    finish(nc, io, dram, out)


def position_table(np):
    pos = np.arange(SEQ, dtype=np.float32)[:, None]
    div = np.exp(np.arange(0, CH, 2, dtype=np.float32) * (-np.log(np.float32(10000.0)) / np.float32(CH)))
    ang = pos * div
    return np.stack([np.sin(ang), np.cos(ang)], axis=-1).reshape(SEQ, CH).T


def interpolation(np):
    pos = np.linspace(0.0, 1.0, CH, dtype=np.float32) * np.float32(LOW - 1)
    i0 = np.clip(np.floor(pos).astype(np.int32), 0, LOW - 2)
    w = pos - i0.astype(np.float32)
    m = np.zeros((CH, LOW), np.float32)
    m[np.arange(CH), i0] = np.float32(1.0) - w
    m[np.arange(CH), i0 + 1] += w
    return m


def kernel(**inputs):
    import numpy as np
    import concourse.bacc as bacc
    from concourse.bass_utils import run_bass_kernel_spmd

    x = np.asarray(inputs["x"])
    side = 14
    px = x.reshape(BATCH, 3, side, 16, side, 16).transpose(0, 1, 3, 5, 2, 4)
    patches = px.reshape(BATCH, KP, 128, IMG).transpose(0, 2, 1, 3)
    index = np.zeros((BATCH, SEQ), np.int32)
    index[:, IMG:] = np.asarray(inputs["x_txt"])
    arrays = {
        "patches": patches,
        "index": index.reshape(BATCH, TP, TILES),
        "table": np.asarray(inputs["L0_txt_w"]),
        "tok_w": np.asarray(inputs["L0_tok_w"]).T.reshape(KP, 128, CH).transpose(1, 0, 2),
        "w_qkv": np.asarray(inputs["L0_attn_Wqkv"]),
        "w_pos": np.asarray(inputs["L0_attn_Wpos"]),
        "pe_t": position_table(np),
        "cols": np.stack([np.asarray(inputs["L0_tok_b"]), np.asarray(inputs["L0_attn_u_bias"]).reshape(-1),
                          np.asarray(inputs["L0_attn_v_bias"]).reshape(-1)], axis=1),
        "ident": np.eye(128, dtype=np.float32),
        "w_proj": np.asarray(inputs["L0_attn_Wproj"]),
        "b_proj": np.asarray(inputs["L0_attn_bproj"]),
        "interp_t": interpolation(np),
        "fc1_t": np.asarray(inputs["L0_ffn_fc1_w"]).T,
        "fc1_b": np.asarray(inputs["L0_ffn_fc1_b"]).reshape(HID // 128, 128).T,
        "fc2_t": np.asarray(inputs["L0_ffn_fc2_w"]).T.reshape(HID // 128, 128, LOW).transpose(1, 0, 2),
        "fc2_b": np.asarray(inputs["L0_ffn_fc2_b"]),
    }
    arrays = {name: np.ascontiguousarray(a) for name, a in arrays.items()}
    nc = bacc.Bacc("TRN2", target_bir_lowering=False, num_devices=1)
    io = {name: nc.dram_tensor(name, a.shape, mybir.dt.from_np(a.dtype), kind="ExternalInput").ap()
          for name, a in arrays.items()}
    out = nc.dram_tensor("out", (BATCH, SEQ, CH), F32, kind="ExternalOutput").ap()
    layer(nc, io, out)
    return run_bass_kernel_spmd(nc, [arrays], core_ids=[0]).results[0]["out"]
```

```python
from contextlib import ExitStack

import concourse.bass as bass
from concourse import mybir

F32 = mybir.dt.float32
BF16 = mybir.dt.bfloat16
I32 = mybir.dt.int32
ALU = mybir.AluOpType
ACT = mybir.ActivationFunctionType
AXIS_X = mybir.AxisListType.X

BATCH = 8
CH = 128
HEADS = 8
DH = CH // HEADS
IMG = 196
TXT = 512
SEQ = IMG + TXT
TILES = 6
TP = SEQ // TILES
HALF = SEQ // 2
KP = 6
HID = 512
LOW = CH // 2
EPS = 1e-5
SCALE = DH**-0.5

GROUP = 4
ROWS = 120
STEPS = 6
SLOTS = 6
Q_PARTS = (0, 0, 0, 1, 1, 2)
K_PARTS = (0, 1, 2, 0, 1, 0)
PACKED = SLOTS * DH
VW = 32
UNITS = HEADS // GROUP


def rows_of(t):
    return min(ROWS, SEQ - t * ROWS)


class Tally:

    def __init__(self, sem, per, before=0):
        self.sem, self.per, self.before, self.n = sem, per, before, 0

    def start(self, it):
        self.base, self.n = it * self.per + self.before, 0

    def inc(self, instruction):
        instruction.then_inc(self.sem, 1)
        self.n += 1
        return self.base + self.n

    def close(self):
        assert self.n == self.per, (self.n, self.per)


def alone(eng):
    eng.nop(nofuse=True)


def tiles3(ap, width):
    return ap[:, :, 0:3 * width].rearrange("p a (b c) -> p a b c", b=3)


def spread(ap, n):
    return ap.unsqueeze(2).broadcast_to([ap.shape[0], ap.shape[1], n])


def spread_to(ap, shape, axis):
    return ap.unsqueeze(axis).broadcast_to(shape)


SIDE = {"emb": 1, "emb_turn": 2, "norm_turn": 2, "proj": 4, "v": 2, "heads": 3, "back": 2, "out": 2,
        "low": 1, "fc1": 4, "fc2": 1}
HALF_TILES = TILES // 2
CHUNKS = HID // 128
LOWS = TILES // 2
SPLITS = (0, 1, 2)
SPLIT_QV, SPLIT_QU, SPLIT_K = SPLITS
SLOTS_U = STEPS * GROUP
SLOTS_B = UNITS * SLOTS_U
STEPS_B = UNITS * STEPS
THIRD = 2 * GROUP
THIRDS_U = SLOTS_U // THIRD
THIRDS_B = UNITS * THIRDS_U
LAG = 2
PV_FROM = 2
COLS = 2 * ROWS
PAIR = 2
RAW_RING = 3
PAIRS_B = SLOTS_B // PAIR
SHIFT_RING = 3

AT_PROJ = (0, 1, 2, 3)
AT_HEADS = (10, 11, 12)
AT_BACK = (14, 15)
AT_OUT = (17, 18)
AT_V = (20, 21)
AT_EMB = 22
AT_EMB_TURN = (24, 25)
AT_LOW = 28
AT_FC1 = (29, 30, 31, 32)
AT_FC2 = (36, 37, 38)
AT_NORM_TURN = (40, 41)
AT_FIRST = (2, 5, 8)
AT_REST = (3, 6, 9)
AT_SECOND = (4, 7, 10)
AT_LAST = (5, 8, 11)
AT_FIN_MEAN, AT_FIN_CENTER, AT_FIN_SQUARE, AT_FIN_VAR, AT_FIN_NORM, AT_FIN_LOW = 19, 20, 22, 23, 25, 26
AT_GELU = 34
AT_MEAN, AT_CENTER, AT_SQUARE, AT_VAR, AT_NORM = 27, 29, 30, 31, 34


def count(b, per, n):
    value = b * per + n
    return None if isinstance(value, int) and value <= 0 else value


def exists(b, n=0, per=1):
    return not isinstance(b, int) or 0 <= b * per + n < BATCH * per


def layer(nc, io, out):
    dram = {name: nc.dram_tensor("scratch_" + name, shape, dt, kind="Internal").ap() for name, shape, dt in (
        ("h", (BATCH, TP, TILES * CH), F32),
        ("qk", (BATCH, 3, 3, CH, SEQ), BF16),
        ("pos", (3, CH, SEQ), BF16),
        ("raw", (UNITS, GROUP, SEQ * (SEQ + 1)), F32),
    )}
    with ExitStack() as ctx:
        def sb(name, shape, dt=F32):
            return ctx.enter_context(nc.sbuf_tensor("s_" + name, shape, dt))

        def psum(name, shape, dt=F32):
            return ctx.enter_context(nc.psum_tensor(name, shape, dt))

        def sem(name):
            return ctx.enter_context(nc.semaphore(name))

        ident = sb("ident", [128, 128])
        pos_pack = sb("pos_pack", [PACKED, HEADS, SEQ], BF16)
        qv_pack = [sb(f"qv_pack{g}", [PACKED, GROUP, SEQ], BF16) for g in range(UNITS)]
        qu_pack = [sb(f"qu_pack{g}", [PACKED, GROUP, SEQ], BF16) for g in range(UNITS)]
        k_pack = [sb(f"k_pack{g}", [PACKED, GROUP, SEQ], BF16) for g in range(UNITS)]
        v_ones = [sb(f"v_ones{g}", [TP, TILES, GROUP, VW]) for g in range(UNITS)]
        raw = [sb(f"raw{i}", [ROWS, PAIR, SEQ + 1]) for i in range(RAW_RING)]
        shifted = [sb(f"shifted{i}", [ROWS, GROUP, SEQ]) for i in range(SHIFT_RING)]
        top = sb("top", [ROWS, GROUP])
        probs_t = [sb(f"probs_t{i}", [128, GROUP, TILES, COLS]) for i in range(2)]
        out_t = [sb(f"out_t{g}", [128, SEQ]) for g in range(UNITS)]
        tok_w = sb("tok_w", [128, KP, CH])
        w_qkv = sb("w_qkv", [CH, 3 * CH])
        cols = sb("cols", [CH, 3])
        w_proj = sb("w_proj", [CH, CH])
        b_proj = sb("b_proj", [TP, CH])
        fc1_b = sb("fc1_b", [128, CHUNKS])
        fc2_t = sb("fc2_t", [128, CHUNKS, LOW])
        fc2_b = sb("fc2_b", [TP, LOW])
        w_up = sb("w_up", [LOW, HID])
        minus_half = sb("minus_half", [TP, TILES])
        early = probs_t[1][:].rearrange("p h j n -> p (h j n)")
        pe_t = early[:, 0:SEQ]
        w_pos = early[:, 720:720 + CH]
        fc1_t = early[:, 1024:1024 + HID]
        interp_t = early[:, 1536:1536 + LOW]
        patches = sb("patches", [128, KP, IMG])
        index = sb("index", [TP, TILES], I32)
        emb_t = sb("emb_t", [CH, IMG])
        h = sb("h", [TP, TILES, CH])
        total, mean, var, rstd = (sb(f"{x}", [TP, TILES]) for x in ("total", "mean", "var", "rstd"))
        normed_all = sb("normed", [128, TILES, CH])
        normed = normed_all[0:TP]
        normed_t = sb("normed_t", [CH, SEQ])
        heads_all = sb("heads", [128, TILES, CH])
        heads = heads_all[0:TP]
        q_x = normed_all[:].rearrange("p j c -> p (j c)")[:, 0:SEQ]
        k_x = heads_all[:].rearrange("p j c -> p (j c)")[:, 0:SEQ]
        rest = sb("rest", [CH, SEQ])
        parts = [sb(f"parts{i}", [CH, 3, SEQ], BF16) for i in range(2)]
        v_rows = sb("v_rows", [TP, TILES, CH])
        fin_h = sb("fin_h", [TP, TILES, CH])
        inv = sb("inv", [TP, 4 * GROUP])
        fin_total, fin_mean, fin_var, fin_rstd = (sb(f"fin_{x}", [TP, TILES]) for x in
                                                  ("total", "mean", "var", "rstd"))
        low = sb("low", [TP, LOWS, LOW])
        low_t = sb("low_t", [LOW, LOWS * TP])
        hidden = sb("hidden", [128, CHUNKS, LOWS * TP])
        flat = hidden[:].rearrange("p c n -> p (c n)")
        heads_n = flat[:, 0:SEQ].rearrange("p (j n) -> p j n", j=TILES)
        pairs = flat[0:TP, SEQ:SEQ + LOWS * CH].rearrange("p (s c) -> p s c", s=LOWS)
        delta = sb("delta", [TP, LOWS, LOW])

        ps_pos = psum("ps_pos", [128, 2, 512])
        ps_key = psum("ps_key", [128, 2, 512])
        ps_turn = psum("ps_turn", [128, 2, 512])
        ps_out = psum("ps_out", [128, 512])
        ps_side = psum("ps_side", [128, 512])

        def three(width):
            return ps_side[:, 0:3 * width].rearrange("p (b c) -> p b c", b=3)

        consts_in = sem("consts_in")
        pos_in = sem("pos_in")
        presets = sem("presets")
        patches_in, index_in, gathered, fin_h_in = (sem(x) for x in (
            "patches_in", "index_in", "gathered", "fin_h_in"))
        qv_in = [sem(f"qv_in{g}") for g in range(UNITS)]
        qu_in = [sem(f"qu_in{g}") for g in range(UNITS)]
        k_in = [sem(f"k_in{g}") for g in range(UNITS)]
        shifted_in = [sem(f"shifted_in{i}") for i in range(SHIFT_RING)]
        pos_stored, h_stored, result_stored = (sem(x) for x in ("pos_stored", "h_stored", "result_stored"))
        parts_stored = [sem(f"parts_stored{i}") for i in range(2)]
        raw_stored = [sem(f"raw_stored{i}") for i in range(RAW_RING)]
        pos_scored = sem("pos_scored")
        pos_read = sem("pos_read")
        key_scored = sem("key_scored")
        summed = sem("summed")
        lowered = sem("lowered")
        turned = sem("turned")
        expd = sem("expd")
        weighed = sem("weighed")
        out_read = sem("out_read")
        filled = {job: sem(f"filled_{job}") for job in SIDE}
        emptied = {job: sem(f"emptied_{job}") for job in SIDE}
        pos_projected, up_done, up_ok = (sem(x) for x in ("pos_projected", "up_done", "up_ok"))
        mean_step, centered_ok, squared, var_ok, rstd_ok, normed_ok = (sem(x) for x in (
            "mean_step", "centered_ok", "squared", "var_ok", "rstd_ok", "normed_ok"))
        first_part = sem("first_part")
        rest_ok = sem("rest_ok")
        second_part = sem("second_part")
        third_part = sem("third_part")
        v_spread = sem("v_spread")
        biased, fin_step, fin_centered, fin_squared, fin_var_ok, fin_rstd_ok, fin_normed = (sem(x) for x in (
            "biased", "fin_step", "fin_centered", "fin_squared", "fin_var_ok", "fin_rstd_ok", "fin_normed"))
        var_step = sem("var_step")
        low_ok, both_ok, activated, result_ok = (sem(x) for x in (
            "low_ok", "both_ok", "activated", "result_ok"))

        def reached(job, b, i=0):
            return count(b, SIDE[job], i + 1)

        block = ctx.enter_context(nc.Block())

        @block.sync
        def _(sp):
            def load_pack(dst, src, parts_of, g, arrived):
                for s, part in enumerate(parts_of):
                    src_heads = src[part, g * GROUP * DH:(g + 1) * GROUP * DH]
                    sp.dma_start(dst[s * DH:(s + 1) * DH], src_heads.rearrange("(h d) n -> d h n", d=DH)
                                 ).then_inc(arrived, 16)

            def load_qv(b, g):
                if (used := count(b, SLOTS_B, SLOTS_U * (g - 1))) is not None:
                    sp.wait_ge(pos_scored, used)
                alone(sp)
                sp.wait_ge(parts_stored[0], count(b, 32, 16))
                alone(sp)
                load_pack(qv_pack[g], dram["qk"][b, SPLIT_QV], Q_PARTS, g, qv_in[g])

            def load_qk(b, g):
                if (used := count(b, SLOTS_B, SLOTS_U * (g - 1))) is not None:
                    sp.wait_ge(key_scored, used)
                alone(sp)
                sp.wait_ge(parts_stored[1], count(b, 16, 16))
                alone(sp)
                load_pack(qu_pack[g], dram["qk"][b, SPLIT_QU], Q_PARTS, g, qu_in[g])
                sp.wait_ge(parts_stored[0], count(b, 32, 32))
                alone(sp)
                load_pack(k_pack[g], dram["qk"][b, SPLIT_K], K_PARTS, g, k_in[g])

            def store_raw(b, k):
                g, t = k // STEPS % UNITS, k % STEPS
                rows = dram["raw"][g].rearrange("h (n w) -> n h w", w=SEQ + 1)[t * ROWS:t * ROWS + rows_of(t)]
                for half in range(2):
                    w = 2 * k + half
                    sp.wait_ge(pos_read, count(b, SLOTS_B, PAIR * (w + 1)))
                    alone(sp)
                    sp.dma_start(rows[:, PAIR * half:PAIR * (half + 1)], raw[w % RAW_RING][0:rows_of(t)]
                                 ).then_inc(raw_stored[w % RAW_RING], 16)

            def load_shifted(b, k):
                g, t = k // STEPS % UNITS, k % STEPS
                if (used := count(b, SLOTS_B, GROUP * (k - SHIFT_RING + 1))) is not None:
                    sp.wait_ge(turned, used)
                alone(sp)
                last = 2 * (k + (1 if t < STEPS - 1 else 0)) + 1
                for w in range(last - RAW_RING + 1, last + 1):
                    sp.wait_ge(raw_stored[w % RAW_RING], count(b, 16 * PAIRS_B // RAW_RING, 16 * (w // RAW_RING + 1)))
                    alone(sp)
                rows = dram["raw"][g, :, SEQ:SEQ * (SEQ + 1)].rearrange("h (n m) -> n h m", m=SEQ)
                sp.dma_start(shifted[k % SHIFT_RING][0:rows_of(t)], rows[t * ROWS:t * ROWS + rows_of(t)]
                             ).then_inc(shifted_in[k % SHIFT_RING], 16)

            for dst, src in ((pe_t, io["pe_t"]), (w_pos, io["w_pos"]), (cols[:], io["cols"]),
                             (tok_w[:], io["tok_w"]), (ident[:], io["ident"]), (w_qkv[:], io["w_qkv"]),
                             (fc1_t, io["fc1_t"]), (interp_t, io["interp_t"]), (w_proj[:], io["w_proj"]),
                             (fc1_b[:], io["fc1_b"]), (fc2_t[:], io["fc2_t"]),
                             (b_proj[:], io["b_proj"].partition_broadcast(TP)),
                             (fc2_b[:], io["fc2_b"].partition_broadcast(TP))):
                sp.dma_start(dst, src).then_inc(consts_in, 16)
            load_qv(0, 0)
            sp.wait_ge(pos_stored, 16)
            for s, part in enumerate(K_PARTS):
                src = dram["pos"][part].rearrange("(h d) n -> d h n", d=DH)
                sp.dma_start(pos_pack[s * DH:(s + 1) * DH], src).then_inc(pos_in, 16)
            load_qv(0, 1)
            load_qk(0, 0)
            for k in range(STEPS):
                store_raw(0, k)
            for k in range(SHIFT_RING - 1):
                load_shifted(0, k)

            def batch(b):
                for k in range(STEPS_B):
                    if exists(b, (k + SHIFT_RING - 1) // STEPS, UNITS):
                        load_shifted(b, k + SHIFT_RING - 1)
                    if exists(b, k // STEPS + 1, UNITS):
                        store_raw(b, k + STEPS)
                    if k == 0:
                        load_qk(b, 1)
                    if k == 4 and exists(b + 1):
                        load_qv(b + 1, 0)
                    if k == 6 and exists(b + 1):
                        load_qv(b + 1, 1)
                    if k == 7 and exists(b + 1):
                        load_qk(b + 1, 0)

            batch(0)
            with sp.Fori(1, BATCH - 2) as b:
                batch(b)
            batch(BATCH - 2)
            batch(BATCH - 1)

        @block.gpsimd
        def _(pool):
            def gather(b):
                if (used := reached("emb", b - 1)) is not None:
                    pool.wait_ge(filled["emb"], used)
                alone(pool)
                pool.dma_start(patches[:], io["patches"][b]).then_inc(patches_in, 16)
                if (used := count(b, 16 * TILES, 0)) is not None:
                    pool.wait_ge(gathered, used)
                alone(pool)
                pool.dma_start(index[:], io["index"][b]).then_inc(index_in, 16)
                if (used := count(b, 1, 0)) is not None:
                    pool.wait_ge(normed_ok, used)
                pool.wait_ge(index_in, count(b, 16, 16))
                alone(pool)
                for j in range(TILES):
                    pool.indirect_dma_start(
                        h[:, j, :], None, io["table"],
                        bass.IndirectOffsetOnAxis(ap=index[:, j:j + 1], axis=0),
                    ).then_inc(gathered, 16)

            def store_h(b):
                pool.wait_ge(emptied["emb_turn"], reached("emb_turn", b, 1))
                alone(pool)
                pool.dma_start(dram["h"][b], h[:]).then_inc(h_stored, 16)

            def inverse_root(b, src, ready, dst, done):
                pool.wait_ge(ready, count(b, 1, 1))
                pool.tensor_tensor(dst[:], src[:], minus_half[:], ALU.pow).then_inc(done, 1)

            def store_parts(b, t):
                pool.wait_ge(third_part, count(b, 3, 1 + t + 1))
                alone(pool)
                pool.dma_start(dram["qk"][b, t].rearrange("s c n -> c s n"), parts[t % 2][:]
                               ).then_inc(parts_stored[t % 2], 16)

            def spread_v(b, g):
                pool.wait_ge(emptied["v"], reached("v", b, 1))
                if (used := count(b, THIRDS_B, THIRDS_U * (g - 1))) is not None:
                    pool.wait_ge(weighed, used)
                alone(pool)
                pool.tensor_copy(v_ones[g][:, :, :, 0:DH],
                                 v_rows[:, :, g * GROUP * DH:(g + 1) * GROUP * DH]
                                 .rearrange("p j (h d) -> p j h d", h=GROUP)).then_inc(v_spread, 1)

            def load_fin_h(b):
                pool.wait_ge(h_stored, count(b, 16, 16))
                alone(pool)
                pool.dma_start(fin_h[:], dram["h"][b]).then_inc(fin_h_in, 16)

            def add_bias(b):
                pool.wait_ge(fin_h_in, count(b, 16, 16))
                pool.tensor_tensor(fin_h[:], fin_h[:], spread_to(b_proj[:], [TP, TILES, CH], 1),
                                   ALU.add).then_inc(biased, 1)

            def store_result(b):
                pool.wait_ge(result_ok, count(b, 1, 1))
                alone(pool)
                pool.dma_start(out[b].rearrange("(p j) c -> p j c", j=TILES), fin_h[:]
                               ).then_inc(result_stored, 16)
                pool.wait_ge(result_stored, count(b, 16, 16))

            def rstd_of_front(b):
                inverse_root(b, var, var_ok, rstd, rstd_ok)

            def rstd_of_finish(b):
                inverse_root(b, fin_var, fin_var_ok, fin_rstd, fin_rstd_ok)

            pool.memset(minus_half[:], -0.5).then_inc(presets, 1)
            gather(0)
            for i in range(RAW_RING):
                pool.memset(raw[i][:, :, 0:1], 0.0).then_inc(presets, 1)
            for g in range(UNITS):
                pool.memset(v_ones[g][:], 1.0).then_inc(presets, 1)
            pool.wait_ge(presets, 1 + RAW_RING + UNITS)
            pool.wait_ge(third_part, 1)
            pool.dma_start(dram["pos"].rearrange("s c n -> c s n"), parts[1][:]).then_inc(pos_stored, 16)
            store_h(0)
            rstd_of_front(0)
            for t in SPLITS:
                store_parts(0, t)
            gather(1)
            spread_v(0, 0)
            store_h(1)
            rstd_of_front(1)
            pool.wait_ge(consts_in, 16 * 13)

            def batch(b):
                before, next_, after = exists(b - 1), exists(b + 1), exists(b + 2)
                if before:
                    load_fin_h(b - 1)
                    add_bias(b - 1)
                if next_:
                    store_parts(b + 1, SPLIT_QV)
                spread_v(b, 1)
                if next_:
                    store_parts(b + 1, SPLIT_QU)
                    store_parts(b + 1, SPLIT_K)
                if after:
                    gather(b + 2)
                if before:
                    rstd_of_finish(b - 1)
                if after:
                    store_h(b + 2)
                    rstd_of_front(b + 2)
                if next_:
                    spread_v(b + 1, 0)
                if before:
                    store_result(b - 1)

            batch(0)
            with pool.Fori(1, BATCH - 2) as b:
                batch(b)
            batch(BATCH - 2)
            batch(BATCH - 1)
            load_fin_h(BATCH - 1)
            add_bias(BATCH - 1)
            rstd_of_finish(BATCH - 1)
            store_result(BATCH - 1)

        @block.tensor
        def _(pe):
            side = {"emptied": None}

            def fill(job, b, i=0):
                if side["emptied"] is not None:
                    pe.wait_ge(*side["emptied"])
                side["emptied"] = (emptied[job], reached(job, b, i))

            def embed(b):
                fill("emb", b)
                pe.wait_ge(patches_in, count(b, 16, 16))
                for c in range(KP):
                    last = pe.matmul(ps_side[:, 0:IMG], tok_w[:, c, :], patches[:, c, :],
                                     start=(c == 0), stop=(c == KP - 1))
                last.then_inc(filled["emb"], 1)

            def turn_embedding(b, a):
                fill("emb_turn", b, a)
                pe.wait_ge(emptied["emb"], reached("emb", b))
                alone(pe)
                for i in range(3):
                    j = 3 * a + i
                    n = (IMG - j + TILES - 1) // TILES
                    last = pe.transpose(three(CH)[0:n, i, :], emb_t[:, j:IMG:TILES], ident[:])
                last.then_inc(filled["emb_turn"], 1)

            def turn_normed(b, a):
                fill("norm_turn", b, a)
                pe.wait_ge(normed_ok, count(b, 1, 1))
                for i in range(3):
                    last = pe.transpose(three(TP)[:, i, :], normed[:, 3 * a + i, :], ident[0:TP, 0:TP])
                last.then_inc(filled["norm_turn"], 1)

            def project(b, i):
                fill("proj", b, i)
                pe.wait_ge(emptied["norm_turn"], reached("norm_turn", b, 1))
                m, a = i // 2, i % 2
                pe.matmul(ps_side[:, 0:HALF], w_qkv[:, m * CH:(m + 1) * CH],
                          normed_t[:, a * HALF:(a + 1) * HALF], start=True, stop=True).then_inc(filled["proj"], 1)

            def project_v(b, a):
                fill("v", b, a)
                pe.wait_ge(emptied["norm_turn"], reached("norm_turn", b, 1))
                for i in range(3):
                    last = pe.matmul(three(CH)[0:TP, i, :], normed_t[:, 3 * a + i:SEQ:TILES],
                                     w_qkv[:, 2 * CH:3 * CH], start=True, stop=True)
                last.then_inc(filled["v"], 1)

            def turn_heads(b, c):
                fill("heads", b, c)
                pe.wait_ge(out_read, count(b, THIRDS_B, THIRDS_B))
                for i in range(2):
                    for g in range(UNITS):
                        at = (i * UNITS + g) * 128
                        last = pe.transpose(ps_side[0:TP, at:at + 128], out_t[g][:, 2 * c + i:SEQ:TILES], ident[:])
                last.then_inc(filled["heads"], 1)

            def turn_back(b, a):
                fill("back", b, a)
                pe.wait_ge(emptied["heads"], reached("heads", b, 2))
                for i in range(3):
                    last = pe.transpose(three(TP)[:, i, :], heads[:, 3 * a + i, :], ident[0:TP, 0:TP])
                last.then_inc(filled["back"], 1)

            def project_out(b, a):
                fill("out", b, a)
                pe.wait_ge(emptied["back"], reached("back", b, 1))
                for i in range(3):
                    last = pe.matmul(three(CH)[0:TP, i, :], heads_n[:, 3 * a + i, :], w_proj[:],
                                     start=True, stop=True)
                last.then_inc(filled["out"], 1)

            def turn_low(b):
                fill("low", b)
                pe.wait_ge(low_ok, count(b, 1, 1))
                alone(pe)
                for s in range(LOWS):
                    last = pe.transpose(ps_side[0:LOW, s * TP:(s + 1) * TP], low[:, s, :], ident[0:TP, 0:TP])
                last.then_inc(filled["low"], 1)

            def widen(b, c):
                fill("fc1", b, c)
                pe.wait_ge(emptied["low"], reached("low", b))
                pe.matmul(ps_side[:, 0:LOWS * TP], w_up[:, c * 128:(c + 1) * 128], low_t[:],
                          start=True, stop=True).then_inc(filled["fc1"], 1)

            def narrow(b, s):
                if s == 0:
                    fill("fc2", b)
                    pe.wait_ge(activated, count(b, 1, 1))
                for c in range(CHUNKS):
                    last = pe.matmul(ps_side[0:TP, s * LOW:(s + 1) * LOW], hidden[:, c, s * TP:(s + 1) * TP],
                                     fc2_t[:, c, :], start=(c == 0), stop=(c == CHUNKS - 1))
                if s == LOWS - 1:
                    last.then_inc(filled["fc2"], 1)

            def score_positions(b, n):
                g, t, hh = n // SLOTS_U % UNITS, n // GROUP % STEPS, n % GROUP
                if t == 0 and hh == 0:
                    pe.wait_ge(qv_in[g], count(b, 16 * SLOTS, 16 * SLOTS * (n // SLOTS_B + 1)))
                if (used := count(b, SLOTS_B, n)) is not None:
                    pe.wait_ge(pos_read, used)
                rows = rows_of(t)
                for a in range(2):
                    last = pe.matmul(ps_pos[0:rows, a, 0:HALF], qv_pack[g][:, hh, t * ROWS:t * ROWS + rows],
                                     pos_pack[:, g * GROUP + hh, a * HALF:(a + 1) * HALF], start=True, stop=True)
                last.then_inc(pos_scored, 1)

            def score_keys(b, n):
                g, t, hh = n // SLOTS_U, n // GROUP % STEPS, n % GROUP
                if t == 0 and hh == 0:
                    pe.wait_ge(qu_in[g], count(b, 16 * SLOTS, 16 * SLOTS))
                    pe.wait_ge(k_in[g], count(b, 16 * SLOTS, 16 * SLOTS))
                if (used := count(b, SLOTS_B, n)) is not None:
                    pe.wait_ge(summed, used)
                rows = rows_of(t)
                for a in range(2):
                    last = pe.matmul(ps_key[0:rows, a, 0:HALF], qu_pack[g][:, hh, t * ROWS:t * ROWS + rows],
                                     k_pack[g][:, hh, a * HALF:(a + 1) * HALF], start=True, stop=True)
                last.then_inc(key_scored, 1)

            def turn(b, n):
                t, hh = n // GROUP % STEPS, n % GROUP
                rows = rows_of(t)
                pe.wait_ge(lowered, count(b, SLOTS_B, n + 1))
                if (used := count(b, SLOTS_B, n)) is not None:
                    pe.wait_ge(expd, used)
                for j in range(TILES):
                    last = pe.transpose(tiles3(ps_turn, ROWS)[0:TP, j // 3, j % 3, 0:rows],
                                        shifted[n // GROUP % SHIFT_RING][0:rows, hh, j:SEQ:TILES],
                                        ident[0:rows, 0:rows])
                last.then_inc(turned, 1)

            def weigh(b, m, j):
                u = m // THIRDS_U
                cols_ = rows_of(m * 2 % STEPS) + rows_of(m * 2 % STEPS + 1)
                if j == 0:
                    pe.wait_ge(expd, count(b, SLOTS_B, THIRD * (m + 1)))
                    if (used := count(b, THIRDS_B, m)) is not None:
                        pe.wait_ge(out_read, used)
                    pe.wait_ge(v_spread, count(b, UNITS, u + 1))
                for hh in range(GROUP):
                    last = pe.matmul(ps_out[hh * VW:(hh + 1) * VW, 0:cols_], v_ones[u % UNITS][:, j, hh, :],
                                     probs_t[m % 2][0:TP, hh, j, 0:cols_], start=(j == 0), stop=(j == TILES - 1))
                if j == TILES - 1:
                    last.then_inc(weighed, 1)

            def tail(b, n):
                if exists(b, n - LAG, SLOTS_B):
                    turn(b, n - LAG)
                j = n % THIRD - PV_FROM
                if 0 <= j < TILES and exists(b, n - THIRD, SLOTS_B):
                    weigh(b, n // THIRD - 1, j)

            def side_jobs(b, n):
                before, next_, after = exists(b - 1), exists(b + 1), exists(b + 2)
                if next_ and n in AT_PROJ:
                    project(b + 1, AT_PROJ.index(n))
                if before and n in AT_HEADS:
                    turn_heads(b - 1, AT_HEADS.index(n))
                if before and n in AT_BACK:
                    turn_back(b - 1, AT_BACK.index(n))
                if before and n in AT_OUT:
                    project_out(b - 1, AT_OUT.index(n))
                if next_ and n in AT_V:
                    project_v(b + 1, AT_V.index(n))
                if after and n == AT_EMB:
                    embed(b + 2)
                if after and n in AT_EMB_TURN:
                    turn_embedding(b + 2, AT_EMB_TURN.index(n))
                if before and n == AT_LOW:
                    turn_low(b - 1)
                if before and n in AT_FC1:
                    widen(b - 1, AT_FC1.index(n))
                if before and n in AT_FC2:
                    narrow(b - 1, AT_FC2.index(n))
                if after and n in AT_NORM_TURN:
                    turn_normed(b + 2, AT_NORM_TURN.index(n))

            def batch(b):
                for n in range(SLOTS_B):
                    if exists(b, n // SLOTS_U + 1, UNITS):
                        score_positions(b, n + SLOTS_U)
                    score_keys(b, n)
                    tail(b, n)
                    side_jobs(b, n)

            def front(b):
                embed(b)
                for a in range(2):
                    turn_embedding(b, a)
                for a in range(2):
                    turn_normed(b, a)

            pe.wait_ge(consts_in, 16 * 13)
            for a in range(2):
                last = pe.matmul(ps_pos[:, a, 0:HALF], w_pos, pe_t[:, a * HALF:(a + 1) * HALF],
                                 start=True, stop=True)
            last.then_inc(pos_projected, 1)
            pe.matmul(ps_key[0:LOW, 0, :], interp_t, fc1_t, start=True, stop=True).then_inc(up_done, 1)
            front(0)
            for i in range(4):
                project(0, i)
            for a in range(2):
                project_v(0, a)
            pe.wait_ge(first_part, 1)
            pe.wait_ge(pos_in, 16 * SLOTS)
            embed(1)
            for n in range(SLOTS_U):
                score_positions(0, n)
                if n in (1, 3):
                    turn_embedding(1, n // 2)
                if n in (20, 21):
                    turn_normed(1, n - 20)
            pe.wait_ge(up_ok, 1)
            batch(0)
            with pe.Fori(1, BATCH - 2) as b:
                side["emptied"] = (emptied["norm_turn"], reached("norm_turn", b + 1, 1))
                batch(b)
            side["emptied"] = (emptied["norm_turn"], reached("norm_turn", BATCH - 1, 1))
            batch(BATCH - 2)
            batch(BATCH - 1)
            last_b = BATCH - 1
            for n in range(SLOTS_B, SLOTS_B + THIRD):
                tail(last_b, n)
            for c in range(3):
                turn_heads(last_b, c)
            for a in range(2):
                turn_back(last_b, a)
            for a in range(2):
                project_out(last_b, a)
            turn_low(last_b)
            for c in range(CHUNKS):
                widen(last_b, c)
            for s in range(LOWS):
                narrow(last_b, s)

        @block.scalar
        def _(act):
            def bias_embedding(b):
                act.wait_ge(filled["emb"], reached("emb", b))
                if (used := reached("emb_turn", b - 1, 1)) is not None:
                    act.wait_ge(filled["emb_turn"], used)
                act.activation(emb_t[:], ps_side[:, 0:IMG], ACT.Identity,
                               bias=cols[:, 0:1]).then_inc(emptied["emb"], 1)

            def square(b):
                act.wait_ge(centered_ok, count(b, 1, 1))
                if (used := count(b, 3, 0)) is not None:
                    act.wait_ge(rest_ok, used)
                if (used := count(b, 1, -2)) is not None:
                    act.wait_ge(both_ok, used)
                act.activation(normed, h[:], ACT.Square).then_inc(squared, 1)

            def take_normed(b, a):
                act.wait_ge(filled["norm_turn"], reached("norm_turn", b, a))
                if (used := count(b, 4, 0)) is not None:
                    act.wait_ge(filled["proj"], used)
                if (used := count(b, 2, 0)) is not None:
                    act.wait_ge(filled["v"], used)
                act.activation(normed_t[:].rearrange("c (p a b) -> c a b p", a=2, b=3)[:, a], three(TP),
                               ACT.Copy).then_inc(emptied["norm_turn"], 1)

            def take_projection(b, i):
                act.wait_ge(filled["proj"], reached("proj", b, i))
                if i == 0:
                    act.wait_ge(filled["norm_turn"], reached("norm_turn", b, 1))
                m, a = i // 2, i % 2
                act.activation((q_x, k_x)[m][:, a * HALF:(a + 1) * HALF], ps_side[:, 0:HALF],
                               ACT.Copy).then_inc(emptied["proj"], 1)

            def first(b, t):
                if (used := count(b, 16 * (1, 2)[t % 2 == 0], 16 * (t == 2))) is not None:
                    act.wait_ge(parts_stored[t % 2], used)
                if t == SPLIT_QU:
                    act.wait_ge(pos_stored, 16)
                act.wait_ge(emptied["proj"], reached("proj", b, 3 if t == SPLIT_K else 1))
                bias = {SPLIT_QV: cols[:, 2:3], SPLIT_QU: cols[:, 1:2], SPLIT_K: 0.0}[t]
                act.activation(parts[t % 2][:, 0, :], k_x if t == SPLIT_K else q_x, ACT.Identity,
                               bias=bias).then_inc(first_part, 1)

            def second(b, t):
                act.wait_ge(rest_ok, count(b, 3, 1 + t + 1))
                act.activation(parts[t % 2][:, 1, :], rest[:], ACT.Copy).then_inc(second_part, 1)

            def take_v(b, a):
                act.wait_ge(filled["v"], reached("v", b, a))
                if (used := count(b, UNITS, 0)) is not None:
                    act.wait_ge(v_spread, used)
                act.activation(v_rows[:, 3 * a:3 * a + 3, :], three(CH)[0:TP], ACT.Copy
                               ).then_inc(emptied["v"], 1)

            def take_back(b, a):
                act.wait_ge(filled["back"], reached("back", b, a))
                act.activation(heads_n[:, 3 * a:3 * a + 3, :], three(TP), ACT.Copy).then_inc(emptied["back"], 1)

            def fin_square(b):
                act.wait_ge(fin_centered, count(b, 1, 1))
                if exists(b + 2):
                    act.wait_ge(rest_ok, count(b, 3, 1 + 8))
                act.activation(normed, heads, ACT.Square).then_inc(fin_squared, 1)

            def take_low(b):
                act.wait_ge(filled["low"], reached("low", b))
                act.activation(low_t[:], ps_side[0:LOW, 0:LOWS * TP], ACT.Copy).then_inc(emptied["low"], 1)

            def gelu(b):
                act.wait_ge(emptied["fc1"], reached("fc1", b, 3))
                act.activation(hidden[:], hidden[:], ACT.Gelu).then_inc(activated, 1)

            def read_positions(b, n):
                w, t, hh = n // PAIR, n // GROUP % STEPS, n % PAIR
                if hh == 0:
                    if (used := count(b, 16 * PAIRS_B // RAW_RING, 16 * (w // RAW_RING))) is not None:
                        act.wait_ge(raw_stored[w % RAW_RING], used)
                act.wait_ge(pos_scored, count(b, SLOTS_B, n + 1))
                rows = rows_of(t)
                act.activation(raw[w % RAW_RING][0:rows, hh, 1:SEQ + 1].rearrange("p (a n) -> p a n", a=2),
                               ps_pos[0:rows, :, 0:HALF], ACT.Copy).then_inc(pos_read, 1)

            def exponentials(b, n):
                m, t, hh = n // THIRD, n // GROUP % STEPS, n % GROUP
                rows = rows_of(t)
                act.wait_ge(turned, count(b, SLOTS_B, n + 1))
                if n % THIRD == 0:
                    if (used := count(b, THIRDS_B, m - 1)) is not None:
                        act.wait_ge(weighed, used)
                at = t % 2 * ROWS
                act.activation(probs_t[m % 2][0:TP, hh, :, at:at + rows].rearrange("p (a b) n -> p a b n", a=2),
                               tiles3(ps_turn, ROWS)[0:TP, :, :, 0:rows], ACT.Exp, scale=SCALE).then_inc(expd, 1)

            def read_out(b, m):
                g, k = m // THIRDS_U % UNITS, m * 2 % STEPS
                cols_ = rows_of(k) + rows_of(k + 1)
                act.wait_ge(weighed, count(b, THIRDS_B, m + 1))
                if k == 0:
                    if (used := count(b, 3, 3 * (m // THIRDS_B))) is not None:
                        act.wait_ge(filled["heads"], used)
                act.activation(out_t[g][:, k * ROWS:k * ROWS + cols_], ps_out[:, 0:cols_],
                               ACT.Copy).then_inc(out_read, 1)

            def tail(b, n):
                if exists(b, n - LAG, SLOTS_B):
                    exponentials(b, n - LAG)
                if n % THIRD == 0 and exists(b, n - 2 * THIRD, SLOTS_B):
                    read_out(b, n // THIRD - 2)

            def side_jobs(b, n):
                before, next_, after = exists(b - 1), exists(b + 1), exists(b + 2)
                if next_ and n in AT_PROJ:
                    take_projection(b + 1, AT_PROJ.index(n))
                if next_ and n in AT_FIRST:
                    first(b + 1, AT_FIRST.index(n))
                if next_ and n in AT_SECOND:
                    second(b + 1, AT_SECOND.index(n))
                if before and n in AT_BACK:
                    take_back(b - 1, AT_BACK.index(n))
                if next_ and n in AT_V:
                    take_v(b + 1, AT_V.index(n))
                if after and n == AT_EMB:
                    bias_embedding(b + 2)
                if before and n == AT_FIN_SQUARE:
                    fin_square(b - 1)
                if before and n == AT_LOW:
                    take_low(b - 1)
                if after and n == AT_SQUARE:
                    square(b + 2)
                if before and n == AT_GELU:
                    gelu(b - 1)
                if after and n in AT_NORM_TURN:
                    take_normed(b + 2, AT_NORM_TURN.index(n))

            def batch(b):
                for n in range(SLOTS_B):
                    if exists(b, n // SLOTS_U + 1, UNITS):
                        read_positions(b, n + SLOTS_U)
                    tail(b, n)
                    side_jobs(b, n)

            act.wait_ge(consts_in, 16 * 13)
            act.wait_ge(pos_projected, 1)
            pos_x = rest[:].rearrange("c (a n) -> c a n", a=2)
            act.activation(parts[1][:, 0, :].rearrange("c (a n) -> c a n", a=2), ps_pos[:, :, 0:HALF],
                           ACT.Copy)
            act.activation(pos_x, ps_pos[:, :, 0:HALF], ACT.Copy).then_inc(first_part, 1)
            act.wait_ge(up_done, 1)
            act.activation(w_up[:], ps_key[0:LOW, 0, :], ACT.Copy, scale=0.5).then_inc(up_ok, 1)
            act.wait_ge(rest_ok, 1)
            act.activation(parts[1][:, 1, :], rest[:], ACT.Copy).then_inc(second_part, 1)
            bias_embedding(0)
            square(0)
            for a in range(2):
                take_normed(0, a)
            for i in range(4):
                take_projection(0, i)
            for t in SPLITS:
                first(0, t)
                second(0, t)
            for a in range(2):
                take_v(0, a)
            bias_embedding(1)
            act.wait_ge(presets, 1 + RAW_RING + UNITS)
            for n in range(SLOTS_U):
                read_positions(0, n)
                if n == 12:
                    square(1)
                if n in (20, 21):
                    take_normed(1, n - 20)
            batch(0)
            with act.Fori(1, BATCH - 2) as b:
                batch(b)
            batch(BATCH - 2)
            batch(BATCH - 1)
            last_b = BATCH - 1
            for n in range(SLOTS_B, SLOTS_B + THIRD + 1):
                tail(last_b, n)
            for a in range(2):
                take_back(last_b, a)
            fin_square(last_b)
            take_low(last_b)
            gelu(last_b)

        @block.vector
        def _(dve):
            means = Tally(mean_step, 2)
            fin = Tally(fin_step, 8)

            def place_embedding(b, a):
                dve.wait_ge(gathered, count(b, 16 * TILES, 16 * TILES))
                dve.wait_ge(filled["emb_turn"], reached("emb_turn", b, a))
                whole = IMG // TILES
                if a == 0:
                    last = dve.tensor_copy(h[0:whole + 1, 0:3, :], three(CH)[0:whole + 1])
                else:
                    dve.tensor_copy(h[0:whole, 3:6, :], three(CH)[0:whole])
                    rest_tiles = IMG % TILES - 3
                    last = dve.tensor_copy(h[whole:whole + 1, 3:3 + rest_tiles, :],
                                           three(CH)[whole:whole + 1, 0:rest_tiles])
                last.then_inc(emptied["emb_turn"], 1)

            def means_of(b):
                means.start(b)
                dve.wait_ge(emptied["emb_turn"], reached("emb_turn", b, 1))
                m = means.inc(dve.reduce_sum(total[:], h[:], AXIS_X))
                dve.wait_ge(mean_step, m)
                means.inc(dve.tensor_scalar(mean[:], total[:], 1.0 / CH, None, ALU.mult))
                means.close()

            def center(b):
                dve.wait_ge(mean_step, count(b, 2, 2))
                dve.wait_ge(h_stored, count(b, 16, 16))
                dve.tensor_tensor(h[:], h[:], spread(mean[:], CH), ALU.subtract).then_inc(centered_ok, 1)

            def variance(b):
                dve.wait_ge(squared, count(b, 1, 1))
                dve.reduce_sum(total[:], normed, AXIS_X).then_inc(var_step, 1)
                dve.wait_ge(var_step, count(b, 1, 1))
                dve.tensor_scalar(var[:], total[:], 1.0 / CH, EPS, ALU.mult, ALU.add).then_inc(var_ok, 1)

            def normalize(b):
                dve.wait_ge(rstd_ok, count(b, 1, 1))
                dve.tensor_tensor(normed, h[:], spread(rstd[:], CH), ALU.mult).then_inc(normed_ok, 1)

            def take_rest(b, t):
                dve.wait_ge(first_part, count(b, 3, 1 + t + 1))
                dve.wait_ge(third_part, count(b, 3, 1 + t))
                if t == SPLIT_K:
                    ins = dve.tensor_tensor(rest[:], k_x, parts[0][:, 0, :], ALU.subtract)
                else:
                    bias = {SPLIT_QV: cols[:, 2:3], SPLIT_QU: cols[:, 1:2]}[t]
                    ins = dve.scalar_tensor_tensor(out=rest[:], in0=q_x, scalar=bias, in1=parts[t % 2][:, 0, :],
                                                   op0=ALU.add, op1=ALU.subtract)
                ins.then_inc(rest_ok, 1)

            def third(b, t):
                dve.wait_ge(second_part, count(b, 3, 1 + t + 1))
                dve.tensor_tensor(parts[t % 2][:, 2, :], rest[:], parts[t % 2][:, 1, :],
                                  ALU.subtract).then_inc(third_part, 1)

            def divide_heads(b, c):
                if c == 0:
                    fin.start(b)
                    if exists(b + 2):
                        dve.wait_ge(rest_ok, count(b, 3, 1 + 9))
                dve.wait_ge(filled["heads"], reached("heads", b, c))
                src = ps_side[0:TP].rearrange("p (x w) -> p x w", w=VW)
                m = fin.inc(dve.reciprocal(inv[:], src[:, :, DH]))
                dve.wait_ge(fin_step, m)
                dve.tensor_tensor(heads[:, 2 * c:2 * c + 2, :].rearrange("p j (x d) -> p (j x) d", d=DH),
                                  src[:, :, 0:DH], spread(inv[:], DH), ALU.mult).then_inc(emptied["heads"], 1)

            def add_projection(b, a):
                dve.wait_ge(biased, count(b, 1, 1))
                dve.wait_ge(filled["out"], reached("out", b, a))
                dve.tensor_tensor(fin_h[:, 3 * a:3 * a + 3, :], fin_h[:, 3 * a:3 * a + 3, :],
                                  three(CH)[0:TP], ALU.add).then_inc(emptied["out"], 1)

            def fin_means(b):
                dve.wait_ge(emptied["out"], reached("out", b, 1))
                m = fin.inc(dve.reduce_sum(fin_total[:], fin_h[:], AXIS_X))
                dve.wait_ge(fin_step, m)
                fin.inc(dve.tensor_scalar(fin_mean[:], fin_total[:], 1.0 / CH, None, ALU.mult))

            def fin_center(b):
                dve.wait_ge(fin_step, count(b, fin.per, 5))
                dve.tensor_tensor(heads, fin_h[:], spread(fin_mean[:], CH), ALU.subtract
                                  ).then_inc(fin_centered, 1)

            def fin_variance(b):
                dve.wait_ge(fin_squared, count(b, 1, 1))
                m = fin.inc(dve.reduce_sum(fin_total[:], normed, AXIS_X))
                dve.wait_ge(fin_step, m)
                dve.tensor_scalar(fin_var[:], fin_total[:], 1.0 / CH, EPS, ALU.mult, ALU.add
                                  ).then_inc(fin_var_ok, 1)

            def fin_normalize(b):
                dve.wait_ge(fin_rstd_ok, count(b, 1, 1))
                dve.tensor_tensor(normed, heads, spread(fin_rstd[:], CH), ALU.mult).then_inc(fin_normed, 1)

            def low_band(b):
                dve.wait_ge(fin_normed, count(b, 1, 1))
                y = normed.rearrange("p (s r) c -> p s r c", r=2)
                m = fin.inc(dve.tensor_tensor(pairs, y[:, :, 0, :], y[:, :, 1, :], ALU.add))
                dve.tensor_tensor(fin_h[:], fin_h[:], normed, ALU.add).then_inc(both_ok, 1)
                dve.wait_ge(fin_step, m)
                z = pairs.rearrange("p s (c e) -> p s c e", e=2)
                dve.tensor_tensor(low[:], z[:, :, :, 0], z[:, :, :, 1], ALU.add).then_inc(low_ok, 1)

            def take_fc1(b, c):
                dve.wait_ge(filled["fc1"], reached("fc1", b, c))
                dve.tensor_scalar(hidden[:, c, :], ps_side[:, 0:LOWS * TP], fc1_b[:, c:c + 1], None,
                                  ALU.add).then_inc(emptied["fc1"], 1)

            def result(b):
                dve.wait_ge(filled["fc2"], reached("fc2", b))
                dve.tensor_tensor(delta[:], ps_side[0:TP, 0:LOWS * LOW].rearrange("p (s c) -> p s c", s=LOWS),
                                  spread_to(fc2_b[:], [TP, LOWS, LOW], 1), ALU.add).then_inc(emptied["fc2"], 1)
                dve.wait_ge(emptied["fc2"], reached("fc2", b))
                dve.wait_ge(low_ok, count(b, 1, 1))
                m = fin.inc(dve.scalar_tensor_tensor(out=delta[:], in0=low[:], scalar=-0.5, in1=delta[:],
                                                     op0=ALU.mult, op1=ALU.add))
                dve.wait_ge(fin_step, m)
                dve.wait_ge(both_ok, count(b, 1, 1))
                for r in range(2):
                    quads = fin_h[:].rearrange("p (s r) c -> p s r c", r=2)[:, :, r, :].rearrange(
                        "p s (c e) -> p s c e", e=2)
                    change = delta[:].unsqueeze(3).broadcast_to([TP, LOWS, LOW, 2])
                    last = dve.scalar_tensor_tensor(out=quads, in0=change, scalar=0.5, in1=quads,
                                                    op0=ALU.mult, op1=ALU.add)
                last.then_inc(result_ok, 1)
                fin.close()

            def sum_and_lower(b, n):
                k, t, hh = n // GROUP, n // GROUP % STEPS, n % GROUP
                rows, tile = rows_of(t), shifted[k % SHIFT_RING]
                if hh == 0:
                    dve.wait_ge(shifted_in[k % SHIFT_RING],
                                count(b, 16 * STEPS_B // SHIFT_RING, 16 * (k // SHIFT_RING + 1)))
                dve.wait_ge(key_scored, count(b, SLOTS_B, n + 1))
                alone(dve)
                both = tile[0:rows, hh, :].rearrange("p (a n) -> p a n", a=2)
                dve.tensor_tensor_reduce(out=both, in0=ps_key[0:rows, :, 0:HALF], in1=both, scale=1.0,
                                         scalar=-3.0e38, op0=ALU.add, op1=ALU.max,
                                         accum_out=top[0:rows, hh:hh + 1]).then_inc(summed, 1)
                dve.wait_ge(summed, count(b, SLOTS_B, n + 1))
                dve.tensor_scalar(tile[0:rows, hh, :], tile[0:rows, hh, :], top[0:rows, hh:hh + 1], None,
                                  ALU.subtract).then_inc(lowered, 1)

            def side_jobs(b, n):
                before, next_, after = exists(b - 1), exists(b + 1), exists(b + 2)
                if next_ and n in AT_REST:
                    take_rest(b + 1, AT_REST.index(n))
                if next_ and n in AT_LAST:
                    third(b + 1, AT_LAST.index(n))
                if before and n in AT_HEADS:
                    divide_heads(b - 1, AT_HEADS.index(n))
                if before and n in AT_OUT:
                    add_projection(b - 1, AT_OUT.index(n))
                if before and n == AT_FIN_MEAN:
                    fin_means(b - 1)
                if before and n == AT_FIN_CENTER:
                    fin_center(b - 1)
                if before and n == AT_FIN_VAR:
                    fin_variance(b - 1)
                if after and n in AT_EMB_TURN:
                    place_embedding(b + 2, AT_EMB_TURN.index(n))
                if before and n == AT_FIN_NORM:
                    fin_normalize(b - 1)
                if before and n == AT_FIN_LOW:
                    low_band(b - 1)
                if after and n == AT_MEAN:
                    means_of(b + 2)
                if before and n in AT_FC1:
                    take_fc1(b - 1, AT_FC1.index(n))
                if after and n == AT_CENTER:
                    center(b + 2)
                if after and n == AT_VAR:
                    variance(b + 2)
                if after and n == AT_NORM:
                    normalize(b + 2)
                if before and n == AT_FC2[-1]:
                    result(b - 1)

            def batch(b):
                for n in range(SLOTS_B):
                    sum_and_lower(b, n)
                    side_jobs(b, n)

            def front(b):
                for a in range(2):
                    place_embedding(b, a)
                means_of(b)
                center(b)
                variance(b)
                normalize(b)

            dve.wait_ge(consts_in, 16 * 13)
            dve.wait_ge(first_part, 1)
            dve.tensor_tensor(rest[:], rest[:], parts[1][:, 0, :], ALU.subtract).then_inc(rest_ok, 1)
            dve.wait_ge(second_part, 1)
            dve.tensor_tensor(parts[1][:, 2, :], rest[:], parts[1][:, 1, :], ALU.subtract).then_inc(third_part, 1)
            front(0)
            for t in SPLITS:
                take_rest(0, t)
                third(0, t)
            front(1)
            batch(0)
            with dve.Fori(1, BATCH - 2) as b:
                batch(b)
            batch(BATCH - 2)
            batch(BATCH - 1)
            last_b = BATCH - 1
            for c in range(3):
                divide_heads(last_b, c)
            for a in range(2):
                add_projection(last_b, a)
            fin_means(last_b)
            fin_center(last_b)
            fin_variance(last_b)
            fin_normalize(last_b)
            low_band(last_b)
            for c in range(CHUNKS):
                take_fc1(last_b, c)
            result(last_b)


def position_table(np):
    pos = np.arange(SEQ, dtype=np.float32)[:, None]
    div = np.exp(np.arange(0, CH, 2, dtype=np.float32) * (-np.log(np.float32(10000.0)) / np.float32(CH)))
    ang = pos * div
    return np.stack([np.sin(ang), np.cos(ang)], axis=-1).reshape(SEQ, CH).T


def interpolation(np):
    pos = np.linspace(0.0, 1.0, CH, dtype=np.float32) * np.float32(LOW - 1)
    i0 = np.clip(np.floor(pos).astype(np.int32), 0, LOW - 2)
    w = pos - i0.astype(np.float32)
    m = np.zeros((CH, LOW), np.float32)
    m[np.arange(CH), i0] = np.float32(1.0) - w
    m[np.arange(CH), i0 + 1] += w
    return m


def kernel(**inputs):
    import numpy as np
    import concourse.bacc as bacc
    from concourse.bass_utils import run_bass_kernel_spmd

    x = np.asarray(inputs["x"])
    side = 14
    px = x.reshape(BATCH, 3, side, 16, side, 16).transpose(0, 1, 3, 5, 2, 4)
    patches = px.reshape(BATCH, KP, 128, IMG).transpose(0, 2, 1, 3)
    index = np.zeros((BATCH, SEQ), np.int32)
    index[:, IMG:] = np.asarray(inputs["x_txt"])
    arrays = {
        "patches": patches,
        "index": index.reshape(BATCH, TP, TILES),
        "table": np.asarray(inputs["L0_txt_w"]),
        "tok_w": np.asarray(inputs["L0_tok_w"]).T.reshape(KP, 128, CH).transpose(1, 0, 2),
        "w_qkv": np.asarray(inputs["L0_attn_Wqkv"]),
        "w_pos": np.asarray(inputs["L0_attn_Wpos"]),
        "pe_t": position_table(np),
        "cols": np.stack([np.asarray(inputs["L0_tok_b"]), np.asarray(inputs["L0_attn_u_bias"]).reshape(-1),
                          np.asarray(inputs["L0_attn_v_bias"]).reshape(-1)], axis=1),
        "ident": np.eye(128, dtype=np.float32),
        "w_proj": np.asarray(inputs["L0_attn_Wproj"]),
        "b_proj": np.asarray(inputs["L0_attn_bproj"]),
        "interp_t": interpolation(np),
        "fc1_t": np.asarray(inputs["L0_ffn_fc1_w"]).T,
        "fc1_b": np.asarray(inputs["L0_ffn_fc1_b"]).reshape(HID // 128, 128).T,
        "fc2_t": np.asarray(inputs["L0_ffn_fc2_w"]).T.reshape(HID // 128, 128, LOW).transpose(1, 0, 2),
        "fc2_b": np.asarray(inputs["L0_ffn_fc2_b"]),
    }
    arrays = {name: np.ascontiguousarray(a) for name, a in arrays.items()}
    nc = bacc.Bacc("TRN2", target_bir_lowering=False, num_devices=1)
    io = {name: nc.dram_tensor(name, a.shape, mybir.dt.from_np(a.dtype), kind="ExternalInput").ap()
          for name, a in arrays.items()}
    out = nc.dram_tensor("out", (BATCH, SEQ, CH), F32, kind="ExternalOutput").ap()
    layer(nc, io, out)
    return run_bass_kernel_spmd(nc, [arrays], core_ids=[0]).results[0]["out"]
```

```python
from contextlib import ExitStack

import concourse.bass as bass
from concourse import mybir

F32 = mybir.dt.float32
BF16 = mybir.dt.bfloat16
I32 = mybir.dt.int32
ALU = mybir.AluOpType
ACT = mybir.ActivationFunctionType
AXIS_X = mybir.AxisListType.X

BATCH = 8
CH = 128
HEADS = 8
DH = CH // HEADS
IMG = 196
TXT = 512
SEQ = IMG + TXT
TILES = 6
TP = SEQ // TILES
HALF = SEQ // 2
KP = 6
HID = 512
LOW = CH // 2
EPS = 1e-5
SCALE = DH**-0.5

GROUP = 4
ROWS = 120
STEPS = 6
SLOTS = 6
Q_PARTS = (0, 0, 0, 1, 1, 2)
K_PARTS = (0, 1, 2, 0, 1, 0)
PACKED = SLOTS * DH
EXTRA = 3
VW = 32
UNITS = HEADS // GROUP


def rows_of(t):
    return min(ROWS, SEQ - t * ROWS)


class Tally:

    def __init__(self, sem, per):
        self.sem, self.per, self.n = sem, per, 0

    def start(self, it):
        self.base, self.n = it * self.per, 0

    def inc(self, instruction):
        instruction.then_inc(self.sem, 1)
        self.n += 1
        return self.base + self.n

    def close(self):
        assert self.n == self.per, (self.n, self.per)


def alone(eng):
    eng.nop(nofuse=True)


def tiles3(ap, width):
    return ap[:, :, 0:3 * width].rearrange("p a (b c) -> p a b c", b=3)


def spread(ap, n):
    return ap.unsqueeze(2).broadcast_to([ap.shape[0], ap.shape[1], n])


def spread_to(ap, shape, axis):
    return ap.unsqueeze(axis).broadcast_to(shape)


SIDE = {"emb": 1, "emb_turn": 2, "norm_turn": 2, "proj": 4, "v": 2, "heads": 3, "back": 2, "out": 2,
        "low": 1, "fc1": 4, "fc2": 1}
CHUNKS = HID // 128
LOWS = TILES // 2
SPLITS = (0, 1)
SPLIT_Q, SPLIT_K = SPLITS
SLOTS_U = STEPS * GROUP
SLOTS_B = UNITS * SLOTS_U
HALF_Q = STEPS // 2 * ROWS
STEPS_B = UNITS * STEPS
THIRD = 2 * GROUP
THIRDS_U = SLOTS_U // THIRD
THIRDS_B = UNITS * THIRDS_U
LEAD = 18
LAG = 2
PV_FROM = 2
COLS = 2 * ROWS
PAIR = 2
RAW_RING = 4
PAIRS_B = SLOTS_B // PAIR
SHIFT_RING = 3
EARLY_EMB, EARLY_TURN, EARLY_SQUARE = 4, 8, 16
FIN_STEPS = 8
PRESETS = RAW_RING + 2 * UNITS

AT_PROJ = (4, 5, 27, 29)
AT_HEADS = (9, 10, 11)
AT_BACK = (14, 15)
AT_OUT = (16, 17)
AT_LOW = 26
AT_FC1 = (28, 30, 32, 33)
AT_EMB = (34, 35)
AT_EMB_TURN = (36, 37)
AT_FC2 = (38, 39, 40, 41, 42, 43)
AT_V = (44, 46)
AT_NORM_TURN = (46, 47)
AT_FIRST = (10, 29)
AT_SECOND = (14, 32)
AT_FIN_MEAN, AT_FIN_SQUARE, AT_FIN_VAR, AT_FIN_LOW = 18, 20, 22, 25
AT_GELU = 34
AT_MEAN, AT_SQUARE, AT_VAR = 38, 40, 41


def count(b, per, n):
    value = b * per + n
    return None if isinstance(value, int) and value <= 0 else value


def exists(b, n=0, per=1):
    return not isinstance(b, int) or 0 <= b * per + n < BATCH * per


def layer(nc, io, out):
    dram = {name: nc.dram_tensor("scratch_" + name, shape, dt, kind="Internal").ap() for name, shape, dt in (
        ("raw", (UNITS, GROUP, SEQ * (SEQ + 1)), F32),
    )}
    with ExitStack() as ctx:
        def sb(name, shape, dt=F32):
            return ctx.enter_context(nc.sbuf_tensor("s_" + name, shape, dt))

        def psum(name, shape, dt=F32):
            return ctx.enter_context(nc.psum_tensor(name, shape, dt))

        def sem(name):
            return ctx.enter_context(nc.semaphore(name))

        ident = sb("ident", [128, 128])
        pos_pack = sb("pos_pack", [PACKED + EXTRA, HEADS, SEQ], BF16)
        q_pack = [sb(f"q_pack{g}", [PACKED + EXTRA, GROUP, SEQ], BF16) for g in range(UNITS)]
        k_pack = [sb(f"k_pack{g}", [PACKED, GROUP, SEQ], BF16) for g in range(UNITS)]
        v_ones = [sb(f"v_ones{g}", [TP, TILES, GROUP, VW]) for g in range(UNITS)]
        raw = [sb(f"raw{i}", [ROWS, PAIR, SEQ + 1]) for i in range(RAW_RING)]
        shifted = [sb(f"shifted{i}", [ROWS, GROUP, SEQ]) for i in range(SHIFT_RING)]
        top = sb("top", [ROWS, GROUP])
        probs_t = [sb(f"probs_t{i}", [128, GROUP, TILES, COLS]) for i in range(2)]
        out_t = [sb(f"out_t{g}", [128, SEQ]) for g in range(UNITS)]
        tok_w = sb("tok_w", [128, KP, CH])
        w_qkv = sb("w_qkv", [CH, 3 * CH])
        cols = sb("cols", [CH, 2])
        w_proj = sb("w_proj", [CH, CH])
        b_proj = sb("b_proj", [TP, CH])
        fc1_b = sb("fc1_b", [128, CHUNKS])
        fc2_t = sb("fc2_t", [128, CHUNKS, LOW])
        fc2_b = sb("fc2_b", [TP, LOW])
        w_up = sb("w_up", [LOW, HID])
        minus_half = sb("minus_half", [TP, TILES])
        early = probs_t[1][:].rearrange("p h j n -> p (h j n)")
        pe_t = early[:, 0:SEQ]
        w_pos = early[:, 720:720 + CH]
        fc1_t = early[:, 1024:1024 + HID]
        interp_t = early[:, 1536:1536 + LOW]
        u_heads = early[:, 1600:1600 + HEADS]
        v_heads = early[:, 1608:1608 + HEADS]
        v_less_u = early[:, 1616:1616 + HEADS]
        bias_x = early[0:HEADS, 1632:1632 + SEQ]
        bias_rest = early[0:HEADS, 2352:2352 + SEQ]
        bias_parts = early[0:HEADS, 3840:3840 + SEQ * 3 // 2].bitcast(BF16).rearrange("p (s n) -> p s n", s=3)
        patches = sb("patches", [128, KP, IMG])
        index = sb("index", [TP, TILES], I32)
        emb_t = sb("emb_t", [CH, IMG])
        h, h_next, h_now = (sb(name, [TP, TILES, CH]) for name in ("h", "h_next", "h_now"))
        total, mean, var, rstd = (sb(f"{x}", [TP, TILES]) for x in ("total", "mean", "var", "rstd"))
        normed_all = sb("normed", [128, TILES, CH])
        normed = normed_all[0:TP]
        normed_t = sb("normed_t", [CH, SEQ])
        heads_all = sb("heads", [128, TILES, CH])
        heads = heads_all[0:TP]
        q_x = normed_all[:].rearrange("p j c -> p (j c)")[:, 0:SEQ]
        k_x = heads_all[:].rearrange("p j c -> p (j c)")[:, 0:SEQ]
        scratch = sb("scratch", [128, TILES, CH])
        rest = scratch[:].rearrange("p j c -> p (j c)")[:, 0:SEQ]
        squares = scratch[0:TP]
        pos_rest = early[:, 3072:3072 + SEQ]
        parts = [sb(f"parts{i}", [CH, 3, SEQ], BF16) for i in range(2)]
        v_rows = sb("v_rows", [TP, TILES, CH])
        fin_h = sb("fin_h", [TP, TILES, CH])
        inv = sb("inv", [TP, 4 * GROUP])
        fin_total, fin_mean, fin_var, fin_rstd = (sb(f"fin_{x}", [TP, TILES]) for x in
                                                  ("total", "mean", "var", "rstd"))
        low = sb("low", [TP, LOWS, LOW])
        low_t = sb("low_t", [LOW, LOWS * TP])
        hidden = sb("hidden", [128, CHUNKS, LOWS * TP])
        flat = hidden[:].rearrange("p c n -> p (c n)")
        heads_n = flat[:, 0:SEQ].rearrange("p (j n) -> p j n", j=TILES)
        pairs = flat[0:TP, SEQ:SEQ + LOWS * CH].rearrange("p (s c) -> p s c", s=LOWS)
        delta = sb("delta", [TP, LOWS, LOW])

        ps_pos = psum("ps_pos", [128, 2, 512])
        ps_key = psum("ps_key", [128, 2, 512])
        ps_turn = psum("ps_turn", [128, 2, 512])
        ps_out = psum("ps_out", [128, 512])
        ps_side = psum("ps_side", [128, 512])

        free = [ps_pos[:, 0], ps_pos[:, 1], ps_key[:, 0], ps_key[:, 1]]
        free_fc2 = [ps_side[:], ps_turn[:, 0], ps_turn[:, 1]]

        def three(width, bank=None):
            bank = ps_side[:] if bank is None else bank
            return bank[:, 0:3 * width].rearrange("p (b c) -> p b c", b=3)

        consts_in, more_consts_in, finish_consts_in = (sem(x) for x in (
            "consts_in", "more_consts_in", "finish_consts_in"))
        pos_in = sem("pos_in")
        presets = sem("presets")
        minus_half_ok = sem("minus_half_ok")
        patches_in, index_in, gathered = (sem(x) for x in ("patches_in", "index_in", "gathered"))
        q_in = [[sem(f"q_in{g}_{half}") for half in range(2)] for g in range(UNITS)]
        k_in = [sem(f"k_in{g}") for g in range(UNITS)]
        shifted_in = [sem(f"shifted_in{i}") for i in range(SHIFT_RING)]
        result_stored = sem("result_stored")
        raw_stored = [sem(f"raw_stored{i}") for i in range(RAW_RING)]
        pos_scored = sem("pos_scored")
        pos_read = sem("pos_read")
        key_scored = sem("key_scored")
        summed = sem("summed")
        lowered = sem("lowered")
        turned = sem("turned")
        expd = sem("expd")
        weighed = sem("weighed")
        out_read = sem("out_read")
        filled = {job: sem(f"filled_{job}") for job in SIDE}
        emptied = {job: sem(f"emptied_{job}") for job in SIDE}
        pos_projected, up_done, up_ok = (sem(x) for x in ("pos_projected", "up_done", "up_ok"))
        mean_step, centered_ok, squared, var_ok, rstd_ok, normed_ok = (sem(x) for x in (
            "mean_step", "centered_ok", "squared", "var_ok", "rstd_ok", "normed_ok"))
        h_kept, h_moved = sem("h_kept"), sem("h_moved")
        less_u_ok = sem("less_u_ok")
        bias_made = sem("bias_made")
        bias_step = sem("bias_step")
        bias_parted = sem("bias_parted")
        first_part = sem("first_part")
        rest_ok = sem("rest_ok")
        second_part = sem("second_part")
        third_part = sem("third_part")
        v_spread = sem("v_spread")
        biased, fin_step, fin_centered, fin_squared, fin_var_ok, fin_rstd_ok, fin_normed = (sem(x) for x in (
            "biased", "fin_step", "fin_centered", "fin_squared", "fin_var_ok", "fin_rstd_ok", "fin_normed"))
        var_step = sem("var_step")
        low_ok = sem("low_ok")
        both_ok = sem("both_ok")
        activated = sem("activated")
        result_ok = sem("result_ok")

        def reached(job, b, i=0):
            return count(b, SIDE[job], i + 1)

        block = ctx.enter_context(nc.Block())

        @block.sync
        def _(sp):
            def load_pack(dst, src, parts_of, g, at, arrived):
                for s, part in enumerate(parts_of):
                    sp.dma_start(dst[s * DH:(s + 1) * DH, :, at], src[g * GROUP * DH:(g + 1) * GROUP * DH, part, at]
                                 ).then_inc(arrived, 16)

            def load_q(b, g, half):
                used_by = SLOTS_U * (g - UNITS) + SLOTS_U // 2 * (half + 1)
                if (used := count(b, SLOTS_B, used_by)) is not None:
                    sp.wait_ge(key_scored, used)
                    alone(sp)
                sp.wait_ge(third_part, count(b, 2, 2))
                alone(sp)
                at = slice(0, HALF_Q) if half == 0 else slice(HALF_Q, SEQ)
                load_pack(q_pack[g], parts[SPLIT_Q], Q_PARTS, g, at, q_in[g][half])

            def load_k(b, g):
                if (used := count(b, SLOTS_B, SLOTS_U * (g - 1))) is not None:
                    sp.wait_ge(key_scored, used)
                    alone(sp)
                sp.wait_ge(third_part, count(b, 2, 3))
                alone(sp)
                load_pack(k_pack[g], parts[SPLIT_K], K_PARTS, g, slice(0, SEQ), k_in[g])

            def load_shifted(b, k):
                g, t = k // STEPS % UNITS, k % STEPS
                if (used := count(b, SLOTS_B, GROUP * (k - SHIFT_RING + 1))) is not None:
                    sp.wait_ge(turned, used)
                alone(sp)
                last = 2 * (k + (1 if t < STEPS - 1 else 0)) + 1
                for w in range(last - RAW_RING + 1, last + 1):
                    sp.wait_ge(raw_stored[w % RAW_RING], count(b, 16 * PAIRS_B // RAW_RING, 16 * (w // RAW_RING + 1)))
                    alone(sp)
                rows = dram["raw"][g, :, SEQ:SEQ * (SEQ + 1)].rearrange("h (n m) -> n h m", m=SEQ)
                sp.dma_start(shifted[k % SHIFT_RING][0:rows_of(t)], rows[t * ROWS:t * ROWS + rows_of(t)]
                             ).then_inc(shifted_in[k % SHIFT_RING], 16)

            for dst, src in ((tok_w[:], io["tok_w"]), (cols[:], io["cols"]), (ident[:], io["ident"])):
                sp.dma_start(dst, src).then_inc(consts_in, 16)
            for dst, src in ((pe_t, io["pe_t"]), (w_pos, io["w_pos"]), (u_heads, io["u_heads"]),
                             (v_heads, io["v_heads"]), (w_qkv[:], io["w_qkv"])):
                sp.dma_start(dst, src).then_inc(more_consts_in, 16)
            for dst, src in ((fc1_t, io["fc1_t"]), (interp_t, io["interp_t"]), (w_proj[:], io["w_proj"]),
                             (fc1_b[:], io["fc1_b"]), (fc2_t[:], io["fc2_t"]),
                             (b_proj[:], io["b_proj"].partition_broadcast(TP)),
                             (fc2_b[:], io["fc2_b"].partition_broadcast(TP))):
                sp.dma_start(dst, src).then_inc(finish_consts_in, 16)
            sp.wait_ge(third_part, 1)
            for g in range(UNITS):
                load_pack(pos_pack[:, g * GROUP:(g + 1) * GROUP], parts[1], K_PARTS, g, slice(0, SEQ), pos_in)
            sp.wait_ge(bias_parted, 2)
            for part in range(EXTRA):
                sp.dma_start(pos_pack[PACKED + part:PACKED + part + 1], bias_parts[:, part, :]).then_inc(pos_in, 16)
            for half in range(2):
                load_q(0, 0, half)
            load_k(0, 0)
            for half in range(2):
                load_q(0, 1, half)
            for k in range(SHIFT_RING - 1):
                load_shifted(0, k)

            def batch(b):
                for k in range(STEPS_B):
                    if exists(b, (k + SHIFT_RING - 1) // STEPS, UNITS):
                        load_shifted(b, k + SHIFT_RING - 1)
                    if k == 0 and not (isinstance(b, int) and b == 0):
                        load_q(b, 1, 1)
                    if k == 1:
                        load_k(b, 1)
                    if k == 3 and exists(b + 1):
                        load_q(b + 1, 0, 0)
                    if k == 6 and exists(b + 1):
                        load_q(b + 1, 0, 1)
                    if k == 9 and exists(b + 1):
                        load_q(b + 1, 1, 0)
                        load_k(b + 1, 0)

            batch(0)
            with sp.Fori(1, BATCH - 2) as b:
                batch(b)
            batch(BATCH - 2)
            batch(BATCH - 1)

        @block.gpsimd
        def _(pool):
            def gather(b):
                if (used := count(b, 16 * TILES, 0)) is not None:
                    pool.wait_ge(gathered, used)
                alone(pool)
                pool.dma_start(index[:], io["index"][b]).then_inc(index_in, 16)
                if (used := reached("emb", b - 1)) is not None:
                    pool.wait_ge(filled["emb"], used)
                alone(pool)
                pool.dma_start(patches[:], io["patches"][b]).then_inc(patches_in, 16)
                if (used := count(b, 1, 0)) is not None:
                    pool.wait_ge(centered_ok, used)
                    pool.wait_ge(h_kept, used)
                pool.wait_ge(index_in, count(b, 16, 16))
                alone(pool)
                for j in range(TILES):
                    pool.indirect_dma_start(
                        h[:, j, :], None, io["table"],
                        bass.IndirectOffsetOnAxis(ap=index[:, j:j + 1], axis=0),
                    ).then_inc(gathered, 16)

            def keep_h(b):
                pool.wait_ge(emptied["emb_turn"], reached("emb_turn", b, 1))
                if (used := count(b, 1, 0)) is not None:
                    pool.wait_ge(h_moved, used)
                alone(pool)
                pool.tensor_copy(h_next[:], h[:]).then_inc(h_kept, 1)

            def move_h(b):
                pool.wait_ge(h_kept, count(b, 1, 1))
                if (used := count(b, 1, 0)) is not None:
                    pool.wait_ge(biased, used)
                alone(pool)
                pool.tensor_copy(h_now[:], h_next[:]).then_inc(h_moved, 1)

            def inverse_root(b, src, ready, dst, done):
                pool.wait_ge(ready, count(b, 1, 1))
                pool.tensor_tensor(dst[:], src[:], minus_half[:], ALU.pow).then_inc(done, 1)

            def spread_v(b, g):
                pool.wait_ge(emptied["v"], reached("v", b, 1))
                if (used := count(b, THIRDS_B, THIRDS_U * (g - 1))) is not None:
                    pool.wait_ge(weighed, used)
                alone(pool)
                pool.tensor_copy(v_ones[g][:, :, :, 0:DH],
                                 v_rows[:, :, g * GROUP * DH:(g + 1) * GROUP * DH]
                                 .rearrange("p j (h d) -> p j h d", h=GROUP)).then_inc(v_spread, 1)

            def add_bias(b):
                pool.wait_ge(h_moved, count(b, 1, 1))
                pool.tensor_tensor(fin_h[:], h_now[:], spread_to(b_proj[:], [TP, TILES, CH], 1),
                                   ALU.add).then_inc(biased, 1)

            def store_result(b):
                pool.wait_ge(result_ok, count(b, 1, 1))
                alone(pool)
                pool.dma_start(out[b].rearrange("(p j) c -> p j c", j=TILES), fin_h[:]
                               ).then_inc(result_stored, 16)
                pool.wait_ge(result_stored, count(b, 16, 16))

            def split(b, t):
                pool.wait_ge(first_part, count(b, 2, 1 + t + 1))
                pool.wait_ge(third_part, count(b, 2, 1 + t))
                pool.tensor_tensor(rest, (q_x, k_x)[t], parts[t][:, 0, :], ALU.subtract).then_inc(rest_ok, 1)
                pool.wait_ge(second_part, count(b, 2, 1 + t + 1))
                pool.tensor_tensor(parts[t][:, 2, :], rest, parts[t][:, 1, :], ALU.subtract
                                   ).then_inc(third_part, 1)

            def center(b):
                pool.wait_ge(mean_step, count(b, 2, 2))
                if (used := count(b, 1, -2)) is not None:
                    pool.wait_ge(low_ok, used)
                    pool.wait_ge(both_ok, used)
                pool.tensor_tensor(normed, h[:], spread(mean[:], CH), ALU.subtract).then_inc(centered_ok, 1)

            def normalize(b):
                inverse_root(b, var, var_ok, rstd, rstd_ok)
                pool.wait_ge(rstd_ok, count(b, 1, 1))
                pool.tensor_tensor(normed, normed, spread(rstd[:], CH), ALU.mult).then_inc(normed_ok, 1)

            def fin_center(b):
                pool.wait_ge(fin_step, count(b, FIN_STEPS, 5))
                pool.tensor_tensor(heads, fin_h[:], spread(fin_mean[:], CH), ALU.subtract
                                   ).then_inc(fin_centered, 1)

            def fin_normalize(b):
                inverse_root(b, fin_var, fin_var_ok, fin_rstd, fin_rstd_ok)
                pool.wait_ge(fin_rstd_ok, count(b, 1, 1))
                pool.tensor_tensor(normed, heads, spread(fin_rstd[:], CH), ALU.mult).then_inc(fin_normed, 1)
                pool.wait_ge(fin_normed, count(b, 1, 1))
                pool.tensor_tensor(fin_h[:], fin_h[:], normed, ALU.add).then_inc(both_ok, 1)

            gather(0)
            for i in range(RAW_RING):
                pool.memset(raw[i][:, :, 0:1], 0.0).then_inc(presets, 1)
            for g in range(UNITS):
                pool.memset(v_ones[g][:], 1.0).then_inc(presets, 1)
            center(0)
            pool.wait_ge(minus_half_ok, 1)
            normalize(0)
            split(0, SPLIT_Q)
            keep_h(0)
            split(0, SPLIT_K)
            gather(1)
            spread_v(0, 0)
            center(1)
            normalize(1)
            pool.wait_ge(finish_consts_in, 16 * 7)

            def batch(b):
                before, next_, after = exists(b - 1), exists(b + 1), exists(b + 2)
                if before:
                    add_bias(b - 1)
                move_h(b)
                if next_:
                    keep_h(b + 1)
                if after:
                    gather(b + 2)
                if next_:
                    split(b + 1, SPLIT_Q)
                spread_v(b, 1)
                if before:
                    fin_center(b - 1)
                    fin_normalize(b - 1)
                if next_:
                    split(b + 1, SPLIT_K)
                if after:
                    center(b + 2)
                    normalize(b + 2)
                if before:
                    store_result(b - 1)
                if next_:
                    spread_v(b + 1, 0)

            batch(0)
            with pool.Fori(1, BATCH - 2) as b:
                batch(b)
            batch(BATCH - 2)
            batch(BATCH - 1)
            add_bias(BATCH - 1)
            fin_center(BATCH - 1)
            fin_normalize(BATCH - 1)
            store_result(BATCH - 1)

        @block.tensor
        def _(pe):
            side = {"emptied": None}

            def fill(job, b, i=0, bank=None):
                if bank is not None:
                    return bank
                if side["emptied"] is not None:
                    pe.wait_ge(*side["emptied"])
                side["emptied"] = (emptied[job], reached(job, b, i))
                return ps_side[:]

            def embed(b, half):
                if half == 0:
                    fill("emb", b)
                    pe.wait_ge(patches_in, count(b, 16, 16))
                for c in range(half * KP // 2, (half + 1) * KP // 2):
                    last = pe.matmul(ps_side[:, 0:IMG], tok_w[:, c, :], patches[:, c, :],
                                     start=(c == 0), stop=(c == KP - 1))
                if half == 1:
                    last.then_inc(filled["emb"], 1)

            def turn_embedding(b, a):
                fill("emb_turn", b, a)
                pe.wait_ge(emptied["emb"], reached("emb", b))
                alone(pe)
                for i in range(3):
                    j = 3 * a + i
                    n = (IMG - j + TILES - 1) // TILES
                    last = pe.transpose(three(CH)[0:n, i, :], emb_t[:, j:IMG:TILES], ident[:])
                last.then_inc(filled["emb_turn"], 1)

            def turn_normed(b, a):
                fill("norm_turn", b, a)
                pe.wait_ge(normed_ok, count(b, 1, 1))
                for i in range(3):
                    last = pe.transpose(three(TP)[:, i, :], normed[:, 3 * a + i, :], ident[0:TP, 0:TP])
                last.then_inc(filled["norm_turn"], 1)

            def project(b, i):
                fill("proj", b, i)
                pe.wait_ge(emptied["norm_turn"], reached("norm_turn", b, 1))
                m, a = i // 2, i % 2
                pe.matmul(ps_side[:, 0:HALF], w_qkv[:, m * CH:(m + 1) * CH],
                          normed_t[:, a * HALF:(a + 1) * HALF], start=True, stop=True).then_inc(filled["proj"], 1)

            def project_v(b, a):
                fill("v", b, a)
                pe.wait_ge(emptied["norm_turn"], reached("norm_turn", b, 1))
                for i in range(3):
                    last = pe.matmul(three(CH)[0:TP, i, :], normed_t[:, 3 * a + i:SEQ:TILES],
                                     w_qkv[:, 2 * CH:3 * CH], start=True, stop=True)
                last.then_inc(filled["v"], 1)

            def turn_heads(b, c, bank=None):
                bank = fill("heads", b, c, bank)
                pe.wait_ge(out_read, count(b, THIRDS_B, THIRDS_B))
                for i in range(2):
                    for g in range(UNITS):
                        at = (i * UNITS + g) * 128
                        last = pe.transpose(bank[0:TP, at:at + 128], out_t[g][:, 2 * c + i:SEQ:TILES], ident[:])
                last.then_inc(filled["heads"], 1)

            def turn_back(b, a, bank=None):
                bank = fill("back", b, a, bank)
                pe.wait_ge(emptied["heads"], reached("heads", b, 2))
                for i in range(3):
                    last = pe.transpose(three(TP, bank)[:, i, :], heads[:, 3 * a + i, :], ident[0:TP, 0:TP])
                last.then_inc(filled["back"], 1)

            def project_out(b, a, bank=None):
                bank = fill("out", b, a, bank)
                pe.wait_ge(emptied["back"], reached("back", b, 1))
                for i in range(3):
                    last = pe.matmul(three(CH, bank)[0:TP, i, :], heads_n[:, 3 * a + i, :], w_proj[:],
                                     start=True, stop=True)
                last.then_inc(filled["out"], 1)

            def turn_low(b, bank=None):
                bank = fill("low", b, 0, bank)
                pe.wait_ge(low_ok, count(b, 1, 1))
                alone(pe)
                for s in range(LOWS):
                    last = pe.transpose(bank[0:LOW, s * TP:(s + 1) * TP], low[:, s, :], ident[0:TP, 0:TP])
                last.then_inc(filled["low"], 1)

            def widen(b, c, bank=None):
                bank = fill("fc1", b, c, bank)
                pe.wait_ge(emptied["low"], reached("low", b))
                pe.matmul(bank[:, 0:LOWS * TP], w_up[:, c * 128:(c + 1) * 128], low_t[:],
                          start=True, stop=True).then_inc(filled["fc1"], 1)

            def narrow(b, i):
                s, half = i // 2, i % 2
                if i == 0:
                    fill("fc2", b)
                    pe.wait_ge(activated, count(b, 1, 1))
                for c in range(half * CHUNKS // 2, (half + 1) * CHUNKS // 2):
                    last = pe.matmul(ps_side[0:TP, s * LOW:(s + 1) * LOW], hidden[:, c, s * TP:(s + 1) * TP],
                                     fc2_t[:, c, :], start=(c == 0), stop=(c == CHUNKS - 1))
                if i == 2 * LOWS - 1:
                    last.then_inc(filled["fc2"], 1)

            def score_positions(b, n, bank=ps_pos, before=0):
                g, t, hh = n // SLOTS_U % UNITS, n // GROUP % STEPS, n % GROUP
                if t in (0, STEPS // 2) and hh == 0:
                    pe.wait_ge(q_in[g][t // (STEPS // 2)], count(b, 16 * SLOTS, 16 * SLOTS * (n // SLOTS_B + 1)))
                if (used := count(b, SLOTS_B, n - before)) is not None:
                    pe.wait_ge(pos_read, used)
                rows = rows_of(t)
                for a in range(2):
                    last = pe.matmul(bank[0:rows, a, 0:HALF], q_pack[g][:, hh, t * ROWS:t * ROWS + rows],
                                     pos_pack[:, g * GROUP + hh, a * HALF:(a + 1) * HALF], start=True, stop=True)
                last.then_inc(pos_scored, 1)

            def score_keys(b, n):
                g, t, hh = n // SLOTS_U, n // GROUP % STEPS, n % GROUP
                if t == 0 and hh == 0:
                    pe.wait_ge(k_in[g], count(b, 16 * SLOTS, 16 * SLOTS))
                if (used := count(b, SLOTS_B, n)) is not None:
                    pe.wait_ge(summed, used)
                rows = rows_of(t)
                for a in range(2):
                    last = pe.matmul(ps_key[0:rows, a, 0:HALF], q_pack[g][0:PACKED, hh, t * ROWS:t * ROWS + rows],
                                     k_pack[g][:, hh, a * HALF:(a + 1) * HALF], start=True, stop=True)
                last.then_inc(key_scored, 1)

            def turn(b, n):
                t, hh = n // GROUP % STEPS, n % GROUP
                rows = rows_of(t)
                pe.wait_ge(lowered, count(b, SLOTS_B, n + 1))
                if (used := count(b, SLOTS_B, n)) is not None:
                    pe.wait_ge(expd, used)
                for j in range(TILES):
                    last = pe.transpose(tiles3(ps_turn, ROWS)[0:TP, j // 3, j % 3, 0:rows],
                                        shifted[n // GROUP % SHIFT_RING][0:rows, hh, j:SEQ:TILES],
                                        ident[0:rows, 0:rows])
                last.then_inc(turned, 1)

            def weigh(b, m, j):
                u = m // THIRDS_U
                cols_ = rows_of(m * 2 % STEPS) + rows_of(m * 2 % STEPS + 1)
                if j == 0:
                    pe.wait_ge(expd, count(b, SLOTS_B, THIRD * (m + 1)))
                    if (used := count(b, THIRDS_B, m)) is not None:
                        pe.wait_ge(out_read, used)
                    pe.wait_ge(v_spread, count(b, UNITS, u + 1))
                for hh in range(GROUP):
                    last = pe.matmul(ps_out[hh * VW:(hh + 1) * VW, 0:cols_], v_ones[u % UNITS][:, j, hh, :],
                                     probs_t[m % 2][0:TP, hh, j, 0:cols_], start=(j == 0), stop=(j == TILES - 1))
                if j == TILES - 1:
                    last.then_inc(weighed, 1)

            def tail(b, n):
                if exists(b, n - LAG, SLOTS_B):
                    turn(b, n - LAG)
                j = n % THIRD - PV_FROM
                if 0 <= j < TILES and exists(b, n - THIRD, SLOTS_B):
                    weigh(b, n // THIRD - 1, j)

            def side_jobs(b, n):
                before, next_, after = exists(b - 1), exists(b + 1), exists(b + 2)
                if next_ and n in AT_PROJ:
                    project(b + 1, AT_PROJ.index(n))
                if before and n in AT_HEADS:
                    turn_heads(b - 1, AT_HEADS.index(n))
                if before and n in AT_BACK:
                    turn_back(b - 1, AT_BACK.index(n))
                if before and n in AT_OUT:
                    project_out(b - 1, AT_OUT.index(n))
                if after and n in AT_EMB:
                    embed(b + 2, AT_EMB.index(n))
                if after and n in AT_EMB_TURN:
                    turn_embedding(b + 2, AT_EMB_TURN.index(n))
                if before and n == AT_LOW:
                    turn_low(b - 1)
                if before and n in AT_FC1:
                    widen(b - 1, AT_FC1.index(n))
                if before and n in AT_FC2:
                    narrow(b - 1, AT_FC2.index(n))
                if next_ and n in AT_V:
                    project_v(b + 1, AT_V.index(n))
                if after and n in AT_NORM_TURN:
                    turn_normed(b + 2, AT_NORM_TURN.index(n))

            def batch(b):
                for n in range(SLOTS_B):
                    if exists(b, n + LEAD, SLOTS_B):
                        score_positions(b, n + LEAD)
                    score_keys(b, n)
                    tail(b, n)
                    side_jobs(b, n)

            pe.wait_ge(consts_in, 16 * 3)
            for half in range(2):
                embed(0, half)
            pe.wait_ge(more_consts_in, 16 * 5)
            for a in range(2):
                last = pe.matmul(ps_pos[:, a, 0:HALF], w_pos, pe_t[:, a * HALF:(a + 1) * HALF],
                                 start=True, stop=True)
            last.then_inc(pos_projected, 1)
            for a in range(2):
                turn_embedding(0, a)
            pe.wait_ge(less_u_ok, 1)
            pe.wait_ge(first_part, 1)
            for a in range(2):
                last = pe.matmul(ps_turn[0:HEADS, a, 0:HALF], v_less_u, rest[:, a * HALF:(a + 1) * HALF],
                                 start=True, stop=True)
            last.then_inc(bias_made, 1)
            pe.wait_ge(finish_consts_in, 16 * 7)
            pe.matmul(ps_key[0:LOW, 0, :], interp_t, fc1_t, start=True, stop=True).then_inc(up_done, 1)
            for a in range(2):
                turn_normed(0, a)
            for i in range(4):
                project(0, i)
            for a in range(2):
                project_v(0, a)
            pe.wait_ge(pos_in, 16 * (UNITS * SLOTS + EXTRA))
            pe.wait_ge(presets, PRESETS)
            pe.wait_ge(up_ok, 1)
            for n in range(LEAD):
                score_positions(0, n, (ps_pos, ps_key)[n % 2], before=1)
                if n in (EARLY_EMB, EARLY_EMB + 1):
                    embed(1, n - EARLY_EMB)
                if n in (EARLY_TURN, EARLY_TURN + 1):
                    turn_embedding(1, n - EARLY_TURN)
                if n >= LEAD - 2:
                    turn_normed(1, n - LEAD + 2)
            batch(0)
            with pe.Fori(1, BATCH - 2) as b:
                side["emptied"] = (emptied["norm_turn"], reached("norm_turn", b + 1, 1))
                batch(b)
            side["emptied"] = (emptied["norm_turn"], reached("norm_turn", BATCH - 1, 1))
            batch(BATCH - 2)
            batch(BATCH - 1)
            last_b = BATCH - 1
            for n in range(SLOTS_B, SLOTS_B + THIRD):
                tail(last_b, n)
            pe.wait_ge(summed, BATCH * SLOTS_B)
            for c in range(3):
                turn_heads(last_b, c, free[c])
            for a in range(2):
                turn_back(last_b, a, free[(3, 0)[a]])
            for a in range(2):
                project_out(last_b, a, free[1 + a])
            turn_low(last_b, free[3])
            for c in range(CHUNKS):
                widen(last_b, c, free[c])
            for c in range(CHUNKS):
                pe.wait_ge(activated, last_b + c + 1)
                for s in range(LOWS):
                    last = pe.matmul(free_fc2[s][0:TP, 0:LOW], hidden[:, c, s * TP:(s + 1) * TP],
                                     fc2_t[:, c, :], start=(c == 0), stop=(c == CHUNKS - 1))
            last.then_inc(filled["fc2"], 1)

        @block.scalar
        def _(act):
            def bias_embedding(b):
                act.wait_ge(filled["emb"], reached("emb", b))
                if (used := reached("emb_turn", b - 1, 1)) is not None:
                    act.wait_ge(filled["emb_turn"], used)
                act.activation(emb_t[:], ps_side[:, 0:IMG], ACT.Identity,
                               bias=cols[:, 0:1]).then_inc(emptied["emb"], 1)

            def square(b):
                act.wait_ge(centered_ok, count(b, 1, 1))
                act.activation(squares, normed, ACT.Square).then_inc(squared, 1)

            def take_normed(b, a):
                act.wait_ge(filled["norm_turn"], reached("norm_turn", b, a))
                if (used := count(b, 4, 0)) is not None:
                    act.wait_ge(filled["proj"], used)
                if (used := count(b, 2, 0)) is not None:
                    act.wait_ge(filled["v"], used)
                act.activation(normed_t[:].rearrange("c (p a b) -> c a b p", a=2, b=3)[:, a], three(TP),
                               ACT.Copy).then_inc(emptied["norm_turn"], 1)

            def take_projection(b, i):
                act.wait_ge(filled["proj"], reached("proj", b, i))
                if i == 0:
                    act.wait_ge(filled["norm_turn"], reached("norm_turn", b, 1))
                if i == 2:
                    if (used := count(b, 1, -1)) is not None:
                        act.wait_ge(fin_normed, used)
                m, a = i // 2, i % 2
                act.activation((q_x, k_x)[m][:, a * HALF:(a + 1) * HALF], ps_side[:, 0:HALF],
                               ACT.Identity, bias=(cols[:, 1:2], 0.0)[m]).then_inc(emptied["proj"], 1)

            def first(b, t):
                if (used := count(b, 16 * SLOTS, 0)) is not None:
                    for packed in (q_in[0] + q_in[1], k_in)[t]:
                        act.wait_ge(packed, used)
                elif t == SPLIT_K:
                    act.wait_ge(pos_in, 16 * (UNITS * SLOTS + EXTRA))
                act.wait_ge(emptied["proj"], reached("proj", b, (1, 3)[t]))
                act.activation(parts[t][:, 0, :], (q_x, k_x)[t], ACT.Copy).then_inc(first_part, 1)

            def second(b, t):
                act.wait_ge(rest_ok, count(b, 2, 1 + t + 1))
                act.activation(parts[t][:, 1, :], rest, ACT.Copy).then_inc(second_part, 1)

            def take_v(b, a):
                act.wait_ge(filled["v"], reached("v", b, a))
                if (used := count(b, UNITS, 0)) is not None:
                    act.wait_ge(v_spread, used)
                act.activation(v_rows[:, 3 * a:3 * a + 3, :], three(CH)[0:TP], ACT.Copy
                               ).then_inc(emptied["v"], 1)

            def take_back(b, a, bank=None):
                act.wait_ge(filled["back"], reached("back", b, a))
                act.activation(heads_n[:, 3 * a:3 * a + 3, :], three(TP, bank), ACT.Copy
                               ).then_inc(emptied["back"], 1)

            def fin_square(b):
                act.wait_ge(fin_centered, count(b, 1, 1))
                if exists(b + 2):
                    act.wait_ge(rest_ok, count(b, 2, 1 + 5))
                act.activation(normed, heads, ACT.Square).then_inc(fin_squared, 1)

            def take_low(b, bank=ps_side):
                act.wait_ge(filled["low"], reached("low", b))
                act.activation(low_t[:], bank[0:LOW, 0:LOWS * TP], ACT.Copy).then_inc(emptied["low"], 1)

            def gelu(b):
                act.wait_ge(emptied["fc1"], reached("fc1", b, 3))
                act.activation(hidden[:], hidden[:], ACT.Gelu).then_inc(activated, 1)

            def read_positions(b, n, bank=ps_pos):
                w, t, hh = n // PAIR, n // GROUP % STEPS, n % PAIR
                if hh == 0:
                    if (used := count(b, 16 * PAIRS_B // RAW_RING, 16 * (w // RAW_RING))) is not None:
                        act.wait_ge(raw_stored[w % RAW_RING], used)
                act.wait_ge(pos_scored, count(b, SLOTS_B, n + 1))
                rows = rows_of(t)
                act.activation(raw[w % RAW_RING][0:rows, hh, 1:SEQ + 1].rearrange("p (a n) -> p a n", a=2),
                               bank[0:rows, :, 0:HALF], ACT.Copy).then_inc(pos_read, 1)

            def store_raw(b, w):
                g, t, half = w // (2 * STEPS) % UNITS, w // 2 % STEPS, w % 2
                rows = dram["raw"][g].rearrange("h (n w) -> n h w", w=SEQ + 1)[t * ROWS:t * ROWS + rows_of(t)]
                act.wait_ge(pos_read, count(b, SLOTS_B, PAIR * (w + 1)))
                alone(act)
                act.dma_start(rows[:, PAIR * half:PAIR * (half + 1)], raw[w % RAW_RING][0:rows_of(t)]
                              ).then_inc(raw_stored[w % RAW_RING], 16)

            def exponentials(b, n):
                m, t, hh = n // THIRD, n // GROUP % STEPS, n % GROUP
                rows = rows_of(t)
                act.wait_ge(turned, count(b, SLOTS_B, n + 1))
                if n % THIRD == 0:
                    if (used := count(b, THIRDS_B, m - 1)) is not None:
                        act.wait_ge(weighed, used)
                at = t % 2 * ROWS
                act.activation(probs_t[m % 2][0:TP, hh, :, at:at + rows].rearrange("p (a b) n -> p a b n", a=2),
                               tiles3(ps_turn, ROWS)[0:TP, :, :, 0:rows], ACT.Exp, scale=SCALE).then_inc(expd, 1)

            def read_out(b, m):
                g, k = m // THIRDS_U % UNITS, m * 2 % STEPS
                cols_ = rows_of(k) + rows_of(k + 1)
                act.wait_ge(weighed, count(b, THIRDS_B, m + 1))
                if k == 0:
                    if (used := count(b, 3, 3 * (m // THIRDS_B))) is not None:
                        act.wait_ge(filled["heads"], used)
                act.activation(out_t[g][:, k * ROWS:k * ROWS + cols_], ps_out[:, 0:cols_],
                               ACT.Copy).then_inc(out_read, 1)

            def tail(b, n):
                if exists(b, n - LAG, SLOTS_B):
                    exponentials(b, n - LAG)
                if n % THIRD == 0 and exists(b, n - 2 * THIRD, SLOTS_B):
                    read_out(b, n // THIRD - 2)

            def side_jobs(b, n):
                before, next_, after = exists(b - 1), exists(b + 1), exists(b + 2)
                if next_ and n in AT_PROJ:
                    take_projection(b + 1, AT_PROJ.index(n))
                if next_ and n in AT_FIRST:
                    first(b + 1, AT_FIRST.index(n))
                if next_ and n in AT_SECOND:
                    second(b + 1, AT_SECOND.index(n))
                if before and n in AT_BACK:
                    take_back(b - 1, AT_BACK.index(n))
                if next_ and n in AT_V:
                    take_v(b + 1, AT_V.index(n))
                if after and n == AT_EMB[-1]:
                    bias_embedding(b + 2)
                if before and n == AT_FIN_SQUARE:
                    fin_square(b - 1)
                if before and n == AT_LOW:
                    take_low(b - 1)
                if after and n == AT_SQUARE:
                    square(b + 2)
                if before and n == AT_GELU:
                    gelu(b - 1)
                if after and n in AT_NORM_TURN:
                    take_normed(b + 2, AT_NORM_TURN.index(n))

            def batch(b):
                for n in range(SLOTS_B):
                    if exists(b, n + LEAD, SLOTS_B):
                        read_positions(b, n + LEAD)
                    tail(b, n)
                    if n % PAIR == PAIR - 1 and exists(b, n + LEAD, SLOTS_B):
                        store_raw(b, (n + LEAD) // PAIR)
                    side_jobs(b, n)

            act.wait_ge(consts_in, 16 * 3)
            act.activation(minus_half[:], ident[0:TP, 0:TILES], ACT.Copy, scale=0.0, bias=-0.5).then_inc(minus_half_ok, 1)
            bias_embedding(0)
            act.wait_ge(pos_projected, 1)
            pos_x = rest.rearrange("c (a n) -> c a n", a=2)
            act.activation(parts[1][:, 0, :].rearrange("c (a n) -> c a n", a=2), ps_pos[:, :, 0:HALF],
                           ACT.Copy)
            act.activation(pos_x, ps_pos[:, :, 0:HALF], ACT.Copy).then_inc(first_part, 1)
            act.wait_ge(rest_ok, 1)
            act.activation(parts[1][:, 1, :], pos_rest, ACT.Copy).then_inc(second_part, 1)
            act.wait_ge(bias_made, 1)
            act.activation(bias_x.rearrange("c (a n) -> c a n", a=2), ps_turn[0:HEADS, :, 0:HALF], ACT.Copy)
            act.activation(bias_parts[:, 0, :].rearrange("c (a n) -> c a n", a=2), ps_turn[0:HEADS, :, 0:HALF],
                           ACT.Copy).then_inc(bias_parted, 1)
            square(0)
            act.wait_ge(up_done, 1)
            act.activation(w_up[:], ps_key[0:LOW, 0, :], ACT.Copy, scale=0.5).then_inc(up_ok, 1)
            for a in range(2):
                take_normed(0, a)
            for i in range(2):
                take_projection(0, i)
            first(0, SPLIT_Q)
            second(0, SPLIT_Q)
            for i in range(2, 4):
                take_projection(0, i)
            first(0, SPLIT_K)
            second(0, SPLIT_K)
            for a in range(2):
                take_v(0, a)
            act.wait_ge(presets, PRESETS)
            for n in range(LEAD):
                read_positions(0, n, (ps_pos, ps_key)[n % 2])
                if n % PAIR == PAIR - 1:
                    store_raw(0, n // PAIR)
                if n == EARLY_EMB + 1:
                    bias_embedding(1)
                if n == EARLY_SQUARE:
                    square(1)
                if n >= LEAD - 2:
                    take_normed(1, n - LEAD + 2)
            batch(0)
            with act.Fori(1, BATCH - 2) as b:
                batch(b)
            batch(BATCH - 2)
            batch(BATCH - 1)
            last_b = BATCH - 1
            for n in range(SLOTS_B, SLOTS_B + THIRD + 1):
                tail(last_b, n)
            for a in range(2):
                take_back(last_b, a, free[(3, 0)[a]])
            fin_square(last_b)
            take_low(last_b, free[3])
            for c in range(CHUNKS):
                act.wait_ge(filled["fc1"], reached("fc1", last_b, c))
                act.activation(hidden[:, c, :], free[c][:, 0:LOWS * TP], ACT.Gelu,
                               bias=fc1_b[:, c:c + 1]).then_inc(activated, 1)

        @block.vector
        def _(dve):
            means = Tally(mean_step, 2)
            fin = Tally(fin_step, FIN_STEPS)

            def place_embedding(b, a):
                dve.wait_ge(gathered, count(b, 16 * TILES, 16 * TILES))
                dve.wait_ge(filled["emb_turn"], reached("emb_turn", b, a))
                whole = IMG // TILES
                if a == 0:
                    last = dve.tensor_copy(h[0:whole + 1, 0:3, :], three(CH)[0:whole + 1])
                else:
                    dve.tensor_copy(h[0:whole, 3:6, :], three(CH)[0:whole])
                    rest_tiles = IMG % TILES - 3
                    last = dve.tensor_copy(h[whole:whole + 1, 3:3 + rest_tiles, :],
                                           three(CH)[whole:whole + 1, 0:rest_tiles])
                last.then_inc(emptied["emb_turn"], 1)

            def means_of(b):
                means.start(b)
                dve.wait_ge(emptied["emb_turn"], reached("emb_turn", b, 1))
                m = means.inc(dve.reduce_sum(total[:], h[:], AXIS_X))
                dve.wait_ge(mean_step, m)
                means.inc(dve.tensor_scalar(mean[:], total[:], 1.0 / CH, None, ALU.mult))
                means.close()

            def variance(b):
                dve.wait_ge(squared, count(b, 1, 1))
                dve.reduce_sum(total[:], squares, AXIS_X).then_inc(var_step, 1)
                dve.wait_ge(var_step, count(b, 1, 1))
                dve.tensor_scalar(var[:], total[:], 1.0 / CH, EPS, ALU.mult, ALU.add).then_inc(var_ok, 1)

            def divide_heads(b, c, bank=ps_side):
                if c == 0:
                    fin.start(b)
                if c > 0:
                    dve.wait_ge(emptied["heads"], reached("heads", b, c - 1))
                dve.wait_ge(filled["heads"], reached("heads", b, c))
                src = bank[0:TP].rearrange("p (x w) -> p x w", w=VW)
                m = fin.inc(dve.reciprocal(inv[:], src[:, :, DH]))
                dve.wait_ge(fin_step, m)
                dve.tensor_tensor(heads[:, 2 * c:2 * c + 2, :].rearrange("p j (x d) -> p (j x) d", d=DH),
                                  src[:, :, 0:DH], spread(inv[:], DH), ALU.mult).then_inc(emptied["heads"], 1)

            def add_projection(b, a, bank=None):
                dve.wait_ge(biased, count(b, 1, 1))
                dve.wait_ge(filled["out"], reached("out", b, a))
                dve.tensor_tensor(fin_h[:, 3 * a:3 * a + 3, :], fin_h[:, 3 * a:3 * a + 3, :],
                                  three(CH, bank)[0:TP], ALU.add).then_inc(emptied["out"], 1)

            def fin_means(b):
                dve.wait_ge(emptied["out"], reached("out", b, 1))
                m = fin.inc(dve.reduce_sum(fin_total[:], fin_h[:], AXIS_X))
                dve.wait_ge(fin_step, m)
                fin.inc(dve.tensor_scalar(fin_mean[:], fin_total[:], 1.0 / CH, None, ALU.mult))

            def fin_variance(b):
                dve.wait_ge(fin_squared, count(b, 1, 1))
                m = fin.inc(dve.reduce_sum(fin_total[:], normed, AXIS_X))
                dve.wait_ge(fin_step, m)
                dve.tensor_scalar(fin_var[:], fin_total[:], 1.0 / CH, EPS, ALU.mult, ALU.add
                                  ).then_inc(fin_var_ok, 1)

            def low_band(b):
                dve.wait_ge(fin_normed, count(b, 1, 1))
                y = normed.rearrange("p (s r) c -> p s r c", r=2)
                m = fin.inc(dve.tensor_tensor(pairs, y[:, :, 0, :], y[:, :, 1, :], ALU.add))
                dve.wait_ge(fin_step, m)
                z = pairs.rearrange("p s (c e) -> p s c e", e=2)
                dve.tensor_tensor(low[:], z[:, :, :, 0], z[:, :, :, 1], ALU.add).then_inc(low_ok, 1)

            def take_fc1(b, c):
                dve.wait_ge(filled["fc1"], reached("fc1", b, c))
                dve.tensor_scalar(hidden[:, c, :], ps_side[:, 0:LOWS * TP], fc1_b[:, c:c + 1], None,
                                  ALU.add).then_inc(emptied["fc1"], 1)

            def result(b, banks=None):
                dve.wait_ge(filled["fc2"], reached("fc2", b))
                if banks is None:
                    last = dve.tensor_tensor(delta[:], ps_side[0:TP, 0:LOWS * LOW].rearrange(
                        "p (s c) -> p s c", s=LOWS), spread_to(fc2_b[:], [TP, LOWS, LOW], 1), ALU.add)
                else:
                    for s in range(LOWS):
                        last = dve.tensor_tensor(delta[:, s, :], banks[s][0:TP, 0:LOW], fc2_b[:], ALU.add)
                last.then_inc(emptied["fc2"], 1)
                dve.wait_ge(emptied["fc2"], reached("fc2", b))
                dve.wait_ge(low_ok, count(b, 1, 1))
                m = fin.inc(dve.scalar_tensor_tensor(out=delta[:], in0=low[:], scalar=-0.5, in1=delta[:],
                                                     op0=ALU.mult, op1=ALU.add))
                dve.wait_ge(fin_step, m)
                dve.wait_ge(both_ok, count(b, 1, 1))
                for r in range(2):
                    quads = fin_h[:].rearrange("p (s r) c -> p s r c", r=2)[:, :, r, :].rearrange(
                        "p s (c e) -> p s c e", e=2)
                    change = delta[:].unsqueeze(3).broadcast_to([TP, LOWS, LOW, 2])
                    last = dve.scalar_tensor_tensor(out=quads, in0=change, scalar=0.5, in1=quads,
                                                    op0=ALU.mult, op1=ALU.add)
                last.then_inc(result_ok, 1)
                fin.close()

            def sum_and_lower(b, n):
                k, t, hh = n // GROUP, n // GROUP % STEPS, n % GROUP
                rows, tile = rows_of(t), shifted[k % SHIFT_RING]
                if hh == 0:
                    dve.wait_ge(shifted_in[k % SHIFT_RING],
                                count(b, 16 * STEPS_B // SHIFT_RING, 16 * (k // SHIFT_RING + 1)))
                dve.wait_ge(key_scored, count(b, SLOTS_B, n + 1))
                alone(dve)
                both = tile[0:rows, hh, :].rearrange("p (a n) -> p a n", a=2)
                dve.tensor_tensor_reduce(out=both, in0=ps_key[0:rows, :, 0:HALF], in1=both, scale=1.0,
                                         scalar=-3.0e38, op0=ALU.add, op1=ALU.max,
                                         accum_out=top[0:rows, hh:hh + 1]).then_inc(summed, 1)
                dve.wait_ge(summed, count(b, SLOTS_B, n + 1))
                dve.tensor_scalar(tile[0:rows, hh, :], tile[0:rows, hh, :], top[0:rows, hh:hh + 1], None,
                                  ALU.subtract).then_inc(lowered, 1)

            def side_jobs(b, n):
                before, next_, after = exists(b - 1), exists(b + 1), exists(b + 2)
                if before and n in AT_HEADS:
                    divide_heads(b - 1, AT_HEADS.index(n))
                if before and n in AT_OUT:
                    add_projection(b - 1, AT_OUT.index(n))
                if before and n == AT_FIN_MEAN:
                    fin_means(b - 1)
                if before and n == AT_FIN_VAR:
                    fin_variance(b - 1)
                if after and n in AT_EMB_TURN:
                    place_embedding(b + 2, AT_EMB_TURN.index(n))
                if before and n == AT_FIN_LOW:
                    low_band(b - 1)
                if after and n == AT_MEAN:
                    means_of(b + 2)
                if before and n in AT_FC1:
                    take_fc1(b - 1, AT_FC1.index(n))
                if after and n == AT_VAR:
                    variance(b + 2)
                if before and n == AT_FC2[-1]:
                    result(b - 1)

            def batch(b):
                for n in range(SLOTS_B):
                    sum_and_lower(b, n)
                    side_jobs(b, n)

            dve.wait_ge(consts_in, 16 * 3)
            dve.wait_ge(more_consts_in, 16 * 5)
            dve.tensor_tensor(v_less_u, v_heads, u_heads, ALU.subtract).then_inc(less_u_ok, 1)
            for a in range(2):
                place_embedding(0, a)
            dve.wait_ge(first_part, 1)
            dve.tensor_tensor(pos_rest, rest, parts[1][:, 0, :], ALU.subtract).then_inc(rest_ok, 1)
            dve.wait_ge(second_part, 1)
            dve.tensor_tensor(parts[1][:, 2, :], pos_rest, parts[1][:, 1, :], ALU.subtract
                              ).then_inc(third_part, 1)
            means_of(0)
            variance(0)
            dve.wait_ge(bias_parted, 1)
            b = dve.tensor_tensor(bias_rest, bias_x, bias_parts[:, 0, :], ALU.subtract)
            b.then_inc(bias_step, 1)
            dve.wait_ge(bias_step, 1)
            dve.tensor_copy(bias_parts[:, 1, :], bias_rest).then_inc(bias_step, 1)
            dve.wait_ge(bias_step, 2)
            dve.tensor_tensor(bias_parts[:, 2, :], bias_rest, bias_parts[:, 1, :], ALU.subtract
                              ).then_inc(bias_parted, 1)
            for g in range(UNITS):
                dve.memset(q_pack[g][PACKED:PACKED + EXTRA], 1.0).then_inc(presets, 1)
            for a in range(2):
                place_embedding(1, a)
            means_of(1)
            variance(1)
            batch(0)
            with dve.Fori(1, BATCH - 2) as b:
                batch(b)
            batch(BATCH - 2)
            batch(BATCH - 1)
            last_b = BATCH - 1
            for c in range(3):
                divide_heads(last_b, c, free[c])
            for a in range(2):
                add_projection(last_b, a, free[1 + a])
            fin_means(last_b)
            fin_variance(last_b)
            low_band(last_b)
            result(last_b, free_fc2)


def position_table(np):
    pos = np.arange(SEQ, dtype=np.float32)[:, None]
    div = np.exp(np.arange(0, CH, 2, dtype=np.float32) * (-np.log(np.float32(10000.0)) / np.float32(CH)))
    ang = pos * div
    return np.stack([np.sin(ang), np.cos(ang)], axis=-1).reshape(SEQ, CH).T


def interpolation(np):
    pos = np.linspace(0.0, 1.0, CH, dtype=np.float32) * np.float32(LOW - 1)
    i0 = np.clip(np.floor(pos).astype(np.int32), 0, LOW - 2)
    w = pos - i0.astype(np.float32)
    m = np.zeros((CH, LOW), np.float32)
    m[np.arange(CH), i0] = np.float32(1.0) - w
    m[np.arange(CH), i0 + 1] += w
    return m


def by_head(np, bias):
    columns = np.zeros((UNITS, DH, GROUP, HEADS), np.float32)
    for head in range(HEADS):
        columns[head // GROUP, :, head % GROUP, head] = np.asarray(bias)[head]
    return columns.reshape(CH, HEADS)


def channel_first(np, a):
    a = np.asarray(a)
    return a.reshape(*a.shape[:-1], UNITS, GROUP, DH).swapaxes(-1, -2).reshape(a.shape)


def kernel(**inputs):
    import numpy as np
    import concourse.bacc as bacc
    from concourse.bass_utils import run_bass_kernel_spmd

    x = np.asarray(inputs["x"])
    side = 14
    px = x.reshape(BATCH, 3, side, 16, side, 16).transpose(0, 1, 3, 5, 2, 4)
    patches = px.reshape(BATCH, KP, 128, IMG).transpose(0, 2, 1, 3)
    w_qkv = np.asarray(inputs["L0_attn_Wqkv"])
    index = np.zeros((BATCH, SEQ), np.int32)
    index[:, IMG:] = np.asarray(inputs["x_txt"])
    arrays = {
        "patches": patches,
        "index": index.reshape(BATCH, TP, TILES),
        "table": np.asarray(inputs["L0_txt_w"]),
        "tok_w": np.asarray(inputs["L0_tok_w"]).T.reshape(KP, 128, CH).transpose(1, 0, 2),
        "w_qkv": np.concatenate([channel_first(np, w_qkv[:, :CH]), channel_first(np, w_qkv[:, CH:2 * CH]),
                                 w_qkv[:, 2 * CH:]], axis=1),
        "w_pos": channel_first(np, inputs["L0_attn_Wpos"]),
        "pe_t": position_table(np),
        "cols": np.stack([np.asarray(inputs["L0_tok_b"]),
                          channel_first(np, np.asarray(inputs["L0_attn_u_bias"]).reshape(-1))], axis=1),
        "u_heads": by_head(np, inputs["L0_attn_u_bias"]),
        "v_heads": by_head(np, inputs["L0_attn_v_bias"]),
        "ident": np.eye(128, dtype=np.float32),
        "w_proj": np.asarray(inputs["L0_attn_Wproj"]),
        "b_proj": np.asarray(inputs["L0_attn_bproj"]),
        "interp_t": interpolation(np),
        "fc1_t": np.asarray(inputs["L0_ffn_fc1_w"]).T,
        "fc1_b": np.asarray(inputs["L0_ffn_fc1_b"]).reshape(HID // 128, 128).T,
        "fc2_t": np.asarray(inputs["L0_ffn_fc2_w"]).T.reshape(HID // 128, 128, LOW).transpose(1, 0, 2),
        "fc2_b": np.asarray(inputs["L0_ffn_fc2_b"]),
    }
    arrays = {name: np.ascontiguousarray(a) for name, a in arrays.items()}
    nc = bacc.Bacc("TRN2", target_bir_lowering=False, num_devices=1)
    io = {name: nc.dram_tensor(name, a.shape, mybir.dt.from_np(a.dtype), kind="ExternalInput").ap()
          for name, a in arrays.items()}
    out = nc.dram_tensor("out", (BATCH, SEQ, CH), F32, kind="ExternalOutput").ap()
    layer(nc, io, out)
    return run_bass_kernel_spmd(nc, [arrays], core_ids=[0]).results[0]["out"]
```
